# Optimizing a Trainium2 kernel written in Bass

```python
import numpy as np
import jax
import jax.numpy as jnp

def _softmax(x, axis=-1):
    return jax.nn.softmax(x, axis=axis)

def _gelu(x):
    return jax.nn.gelu(x, approximate=True)

def _silu(x):
    return jax.nn.silu(x)

def _sigmoid(x):
    return jax.nn.sigmoid(x)

def _layernorm(x, axis=-1, eps=1e-05):
    m = jnp.mean(x, axis=axis, keepdims=True)
    v = jnp.var(x, axis=axis, keepdims=True)
    return (x - m) / jnp.sqrt(v + eps)

def _scatter_add(tgt, idx, src, axis=0):
    return tgt.at[idx].add(src)

def _segment_sum(src, seg, n):
    return jax.ops.segment_sum(src, seg, n)
kernel_name = 'mk_macaron_d1_jaxref_r8_722041'

def setup_inputs(seed: int=0):
    np.random.seed(seed)
    _w = jnp.asarray

    def _L0_attn_setup():
        import jax, jax.numpy as jnp
        import numpy as np
        import math
        B, T, C = (4, 256, 128)
        H, DQK, DV = (16, 64, 64)
        key = jax.random.key(seed)
        k1, k2, k3, k4, k5 = jax.random.split(key, 5)
        x_q = jax.random.normal(k1, (B, T, C), dtype=jnp.float32)
        w_q = jax.random.normal(k2, (H, DQK, C), dtype=jnp.float32) / math.sqrt(C)
        w_k = jax.random.normal(k3, (H, DQK, C), dtype=jnp.float32) / math.sqrt(C)
        w_v = jax.random.normal(k4, (H, DV, C), dtype=jnp.float32) / math.sqrt(C)
        w_o = jax.random.normal(k5, (DV * H, C), dtype=jnp.float32) / math.sqrt(C)
        return {'x_q': x_q, 'w_q': w_q, 'w_k': w_k, 'w_v': w_v, 'w_o': w_o}
    _L0_attn_in = _L0_attn_setup()

    def _L0_ffn_setup():
        import jax, jax.numpy as jnp
        import numpy as np
        DIM = 128

        def _reference_tuple_inner(x, W_r, W_k, W_v, mu_r, mu_k):
            B, T, C = x.shape
            x_prev = jnp.concatenate([jnp.zeros((B, 1, C), x.dtype), x[:, :-1, :]], axis=1)
            xr = mu_r * x + (1.0 - mu_r) * x_prev
            xk = mu_k * x + (1.0 - mu_k) * x_prev
            r = jax.nn.sigmoid(jnp.einsum('btc,dc->btd', xr, W_r))
            k = jnp.einsum('btc,dc->btd', xk, W_k)
            k_act = jnp.square(jax.nn.relu(k))
            out = r * jnp.einsum('btc,dc->btd', k_act, W_v)
            new_state = x[:, -1, :]
            return (out, new_state)
        key = jax.random.key(seed)
        ks = jax.random.split(key, 6)
        B, T, C = (8, 256, DIM)
        x = jax.random.normal(ks[0], (B, T, C), dtype=jnp.float32)
        s = 1.0 / np.sqrt(C)
        W_r = jax.random.uniform(ks[1], (C, C), jnp.float32, -s, s)
        W_k = jax.random.uniform(ks[2], (C, C), jnp.float32, -s, s)
        W_v = jax.random.uniform(ks[3], (C, C), jnp.float32, -s, s)
        mu_r = jax.random.uniform(ks[4], (C,), jnp.float32)
        mu_k = jax.random.uniform(ks[5], (C,), jnp.float32)
        return {'x': x, 'W_r': W_r, 'W_k': W_k, 'W_v': W_v, 'mu_r': mu_r, 'mu_k': mu_k}
    _L0_ffn_in = _L0_ffn_setup()
    _d = {'L0_attn_x_q': _L0_attn_in['x_q'], 'L0_attn_w_q': _L0_attn_in['w_q'], 'L0_attn_w_k': _L0_attn_in['w_k'], 'L0_attn_w_v': _L0_attn_in['w_v'], 'L0_attn_w_o': _L0_attn_in['w_o'], 'L0_ffn_W_r': _L0_ffn_in['W_r'], 'L0_ffn_W_k': _L0_ffn_in['W_k'], 'L0_ffn_W_v': _L0_ffn_in['W_v'], 'L0_ffn_mu_r': _L0_ffn_in['mu_r'], 'L0_ffn_mu_k': _L0_ffn_in['mu_k']}
    _x0 = _d['L0_attn_x_q']
    _d['L0_attn_x_q'] = jax.random.normal(jax.random.fold_in(jax.random.key(seed), 1), (1, 2048, 128), dtype=_x0.dtype)
    del _x0
    return _d

def reference(L0_attn_x_q, L0_attn_w_q, L0_attn_w_k, L0_attn_w_v, L0_attn_w_o, L0_ffn_W_r, L0_ffn_W_k, L0_ffn_W_v, L0_ffn_mu_r, L0_ffn_mu_k):

    def _L0_attn_ref(x_q, w_q, w_k, w_v, w_o):
        import jax, jax.numpy as jnp
        import numpy as np
        import math
        B, T, C = (4, 256, 128)
        H, DQK, DV = (16, 64, 64)
        q = jnp.einsum('ntc,hdc->nhtd', x_q, w_q)
        k = jnp.einsum('ntc,hdc->nhtd', x_q, w_k)
        v = jnp.einsum('ntc,hdc->nhtd', x_q, w_v)
        a = jnp.einsum('nhtd,nhsd->nhts', q, k) / math.sqrt(q.shape[3])
        t = a.shape[2]
        causal_forbidden = jnp.arange(t)[:, None] < jnp.arange(t)[None, :]
        a = jnp.where(causal_forbidden[None, None], -jnp.inf, a)
        a = jax.nn.softmax(a, axis=3)
        y = jnp.einsum('nhts,nhsd->nthd', a, v).reshape(a.shape[0], t, -1)
        return y @ w_o

    def _L0_ffn_ref(x, W_r, W_k, W_v, mu_r, mu_k):
        import jax, jax.numpy as jnp
        import numpy as np
        DIM = 128

        def _reference_tuple_inner(x, W_r, W_k, W_v, mu_r, mu_k):
            B, T, C = x.shape
            x_prev = jnp.concatenate([jnp.zeros((B, 1, C), x.dtype), x[:, :-1, :]], axis=1)
            xr = mu_r * x + (1.0 - mu_r) * x_prev
            xk = mu_k * x + (1.0 - mu_k) * x_prev
            r = jax.nn.sigmoid(jnp.einsum('btc,dc->btd', xr, W_r))
            k = jnp.einsum('btc,dc->btd', xk, W_k)
            k_act = jnp.square(jax.nn.relu(k))
            out = r * jnp.einsum('btc,dc->btd', k_act, W_v)
            new_state = x[:, -1, :]
            return (out, new_state)
        return _reference_tuple_inner(x, W_r, W_k, W_v, mu_r, mu_k)[0]
    x = L0_attn_x_q
    x = x + 0.5 * _L0_ffn_ref(_layernorm(x, axis=-1), L0_ffn_W_r, L0_ffn_W_k, L0_ffn_W_v, L0_ffn_mu_r, L0_ffn_mu_k)
    x = x + _L0_attn_ref(_layernorm(x, axis=-1), L0_attn_w_q, L0_attn_w_k, L0_attn_w_v, L0_attn_w_o)
    x = x + 0.5 * _L0_ffn_ref(_layernorm(x, axis=-1), L0_ffn_W_r, L0_ffn_W_k, L0_ffn_W_v, L0_ffn_mu_r, L0_ffn_mu_k)
    return x

_drawn_inputs = setup_inputs


def setup_inputs(seed=0):
    import zlib

    import numpy as np

    out = dict(_drawn_inputs(seed))
    spreads = {}
    factors = {'L0_ffn_W_r': 3.316, 'L0_ffn_mu_r': 6.571}
    for name, (base, spread) in spreads.items():
        noise = np.random.default_rng([zlib.crc32(name.encode()), seed]).standard_normal(out[name].shape)
        drawn = base * np.exp(spread * noise) if base else spread * noise
        out[name] = jnp.asarray(drawn.astype(out[name].dtype))
    for name, factor in factors.items():
        out[name] = (out[name] * factor).astype(out[name].dtype)
    return out
```

```python
import numpy as np
import concourse.bass as bass
from concourse import mybir
from contextlib import ExitStack


C = 128
T = 2048
H = 16
D = 64
PAIRS = H // 2
CH = 512
NC = T // CH
TB = 128
BPC = CH // TB
NT = T // TB
EPS = 1e-5
SCALE = D ** -0.5
POOL_FROM = 320

UNITS = [(c, j, max(0, j - BPC * c) * TB) for c in range(NC) for j in range(BPC * (c + 1))]
NU = len(UNITS)
LAST = [UNITS.index((c, BPC * (c + 1) - 1, CH - TB)) for c in range(NC)]
PIECES = [(c, b, a, k) for c in range(NC) for b in range(BPC) for a in range(2) for k in range(c + 1)]
NM = len(PIECES)
LEAD = 42
NP = 4
ST_RING = 3
PROJ, MROW, SUMS, OUTP, RECIP, NORM = "proj", "mrow", "sums", "outp", "recip", "norm"

SIDE = {1: (SUMS, -1, 3, 0), 4: (MROW, 0, 2, 0), 5: (PROJ, 1, 0, 0), 7: (PROJ, 1, 0, 1),
        8: (OUTP, -1, 3, 0), 9: (SUMS, 0, 0, 0), 10: (PROJ, 1, 0, 2), 11: (PROJ, 1, 1, 0),
        13: (PROJ, 1, 1, 1), 14: (PROJ, 1, 1, 2), 15: (OUTP, 0, 0, 0), 16: (SUMS, 0, 1, 0),
        17: (PROJ, 1, 2, 0), 19: (PROJ, 1, 2, 1), 20: (MROW, 0, 3, 0), 21: (PROJ, 1, 2, 2),
        22: (OUTP, 0, 1, 0), 24: (MROW, 1, 0, 0), 25: (SUMS, 0, 2, 0), 31: (OUTP, 0, 2, 0),
        32: (MROW, 1, 1, 0), 33: (PROJ, 1, 3, 0), 35: (PROJ, 1, 3, 1), 36: (PROJ, 1, 3, 2)}
DVE_SIDE = {3: (RECIP, -1, 3, 0), 7: (NORM, -1, 3, 0), 11: (RECIP, 0, 0, 0), 14: (NORM, 0, 0, 0),
            18: (RECIP, 0, 1, 0), 21: (NORM, 0, 1, 0), 27: (RECIP, 0, 2, 0), 30: (NORM, 0, 2, 0)}
SLOTS = sorted(SIDE)
BEFORE = ([(PROJ, 0, c, k) for c in range(2) for k in range(3)] + [("max", 0, 8)] + [(MROW, 0, 0, 0)]
          + [(PROJ, 0, 2, k) for k in range(3)] + [("max", 8, 24)] + [(MROW, 0, 1, 0)]
          + [(PROJ, 0, 3, k) for k in range(3)] + [("max", 24, LEAD)])


class Pair:

    def __init__(self, n, i=None, eng=None, bases=None):
        self.n, self.i, self.eng, self.bases = n, i, eng, bases

    def ahead(self, k):
        return Pair(self.n + k, self.i, self.eng, self.bases)

    def parity(self):
        return self.n % 2

    def count(self, sem, per_pair, index, each=1):
        fixed = (per_pair * self.n + index + 1) * each
        if self.i is None:
            return fixed
        if sem.name not in self.bases:
            self.bases[sem.name] = self.eng.snap(self.i * (2 * per_pair * each))
        return self.bases[sem.name] + fixed


def wait(eng, sem, pair, per_pair, index, each=1):
    n = pair.count(sem, per_pair, index, each)
    if not (isinstance(n, int) and n <= 0):
        eng.wait_ge(sem, n)


def over_pairs(nc, eng, body):
    body(Pair(0))
    with eng.Fori(0, (PAIRS - 2) // 2) as i:
        bases = {}
        body(Pair(1, i, eng, bases))
        body(Pair(2, i, eng, bases))
    body(Pair(PAIRS - 1))


def macaron_kernel(nc, x_t, w_qkv, w_o, w_r, w_k, w_v, mu_r, mu_k, out_t):
    f32, f32r, bf16 = mybir.dt.float32, mybir.dt.float32r, mybir.dt.bfloat16
    ALU, ACT, AX = mybir.AluOpType, mybir.ActivationFunctionType, mybir.AxisListType

    ctx = ExitStack()
    with ctx:
        def sb(name, shape, dt=f32):
            return ctx.enter_context(nc.sbuf_tensor(name, shape, dt))

        def sem(name):
            return ctx.enter_context(nc.semaphore(name))

        x = sb("x", [C, T])
        xh = sb("xh", [C, T], f32r)
        xl = sb("xl", [C, T], f32r)
        keys1 = sb("keys1", [128, 2, NC, 2, CH], f32r)
        keys2 = sb("keys2", [65, 2, NC, 2, CH], f32r)
        qry1 = sb("qry1", [128, NC, 2, CH], f32r)
        qry2 = sb("qry2", [65, NC, 2, CH], f32r)
        vals = sb("vals", [128, 2 * NT, C])
        high = sb("high", [128, 2, 2, CH], f32r)
        low = sb("low", [128, 2, 2, CH], f32r)
        prob = sb("prob", [128, NP, 2, CH])
        part = sb("part", [128, 2, 2, CH])
        yn = sb("yn", [128, CH])
        lrow = sb("lrow", [128, CH])
        rcol = sb("rcol", [128, 8])
        icol = sb("icol", [128, 8])
        irow = sb("irow", [1, 2 * CH])
        yraw = sb("yraw", [128, CH])
        rb = sb("rb", [128, CH])
        w_raw = sb("w_raw", [C, 3 * 128])
        wh = sb("wh", [C, 3 * 128], f32r)
        wl = sb("wl", [C, 3 * 128], f32r)
        wo = sb("wo", [128, 2, C])
        most = sb("most", [128, 2, 8, NC])
        neg = sb("neg", [128, 2, 8])
        mrow = sb("mrow", [8, 128], f32r)
        rinv = sb("rinv", [128, 16])
        rinvh = sb("rinvh", [128, 16], f32r)
        rinvl = sb("rinvl", [128, 16], f32r)
        ident = sb("ident", [128, 128])
        identr = sb("identr", [128, 128], f32r)
        identb = sb("identb", [128, 128], bf16)
        above = sb("above", [128, 128], bf16)
        ones = sb("ones", [128, D])
        mean_w = sb("mean_w", [128, 128])
        eps = sb("eps", [128, 1])
        gate = sb("gate", [128, NU])
        wf = sb("wf", [C, 3, C])
        mu = sb("mu", [C, 2])
        omu = sb("omu", [C, 2])
        pflat = prob[:, :, :, :].rearrange("p s a t -> p (s a t)")
        aflat = part[:, :, :, :].rearrange("p s a t -> p (s a t)")
        vflat = vals[:, :, :].rearrange("p s c -> p (s c)")
        xc, sq = pflat[:, 0:T], pflat[:, T:2 * T]
        xn = vflat[:, T - 1:2 * T]

        ps = ctx.enter_context(nc.psum_tensor("ps", [128, 8, CH], f32))
        misc = ps[:, 7, :]

        s_set = sem("s_set")
        d_x, d_c, d_w, d_wo, d_m, d_out = (sem(n) for n in ("d_x", "d_c", "d_w", "d_wo", "d_m", "d_out"))
        d_in = [sem(f"d_in{c}") for c in range(NC)]
        d_a = [sem(f"d_a{c}") for c in range(NC)]
        l_mean, l_xc, l_sq, l_var, l_std, l_rs, l_sp, l_xn = (
            sem(n) for n in ("l_mean", "l_xc", "l_sq", "l_var", "l_std", "l_rs", "l_sp", "l_xn"))
        l_hi, l_lo, l_t = sem("l_hi"), sem("l_lo"), sem("l_t")
        f_t, f_mix, f_z, f_r, f_ka, f_v, f_x, f_k = (
            sem(n) for n in ("f_t", "f_mix", "f_z", "f_r", "f_ka", "f_v", "f_x", "f_k"))
        s_omu = sem("s_omu")
        s_st, s_mx, s_pv, s_pj, s_mt, s_sum, s_op = (
            sem(n) for n in ("s_st", "s_mx", "s_pv", "s_pj", "s_mt", "s_sum", "s_op"))
        s_ex, s_hv, s_mr, s_lr, s_yr, s_wh = (
            sem(n) for n in ("s_ex", "s_hv", "s_mr", "s_lr", "s_yr", "s_wh"))
        d_l, d_i, d_b = (sem(n) for n in ("d_l", "d_i", "d_b"))
        s_rd, s_nm, s_ac, s_lo, s_rc, s_yn, s_xa, s_wl, s_ri = (
            sem(n) for n in ("s_rd", "s_nm", "s_ac", "s_lo", "s_rc", "s_yn", "s_xa", "s_wl", "s_ri"))
        s_mk, s_pa = sem("s_mk"), sem("s_pa")
        l_t2, l_t3, s_pool = (sem(n) for n in ("l_t2", "l_t3", "s_pool"))

        block = ctx.enter_context(nc.Block())

        def chunk(c):
            return slice(c * CH, (c + 1) * CH)

        def slot_of(u):
            return u % NP

        def st_bank(tile):
            return tile % ST_RING

        @block.sync
        def _(sp):
            for c in range(NC):
                sp.dma_start(x[:, chunk(c)], x_t[:, chunk(c)]).then_inc(d_in[c], 16)
            sp.dma_start(wf[:, 0, :], w_r).then_inc(d_c, 16)
            sp.dma_start(wf[:, 1, :], w_k).then_inc(d_c, 16)
            sp.dma_start(wf[:, 2, :], w_v).then_inc(d_c, 16)
            sp.dma_start(mu[:, 0:1], mu_r).then_inc(d_x, 16)
            sp.dma_start(mu[:, 1:2], mu_k).then_inc(d_x, 16)
            sp.dma_start(w_raw[:, :], w_qkv[0]).then_inc(d_w, 16)
            sp.dma_start(wo[:, 0, :], w_o[0:128, :]).then_inc(d_wo, 16)

            def operands(p, c):
                s, par = c % 2, p.parity()
                wait(sp, s_hv, p, 12, 3 * c + 1)
                wait(sp, s_lo, p, 8, 2 * c + 1)
                wait(sp, s_st, p.ahead(-2), 2 * NU, 2 * NU - 1)
                for a in range(2):
                    rows = slice(D * a, D * a + D)
                    sp.dma_start(keys1[0:D, par, c, a, :].bitcast(f32), high[rows, s, 1, :].bitcast(f32)).then_inc(d_a[c], 16)
                    sp.dma_start(keys1[D:128, par, c, a, :].bitcast(f32), low[rows, s, 1, :].bitcast(f32)).then_inc(d_a[c], 16)
                    sp.dma_start(keys2[0:D, par, c, a, :].bitcast(f32), high[rows, s, 1, :].bitcast(f32)).then_inc(d_a[c], 16)
                wait(sp, s_st, p.ahead(-1), 2 * NU, 2 * LAST[c] + 1)
                for a in range(2):
                    rows = slice(D * a, D * a + D)
                    sp.dma_start(qry1[0:D, c, a, :].bitcast(f32), high[rows, s, 0, :].bitcast(f32)).then_inc(d_a[c], 16)
                    sp.dma_start(qry1[D:128, c, a, :].bitcast(f32), high[rows, s, 0, :].bitcast(f32)).then_inc(d_a[c], 16)
                    sp.dma_start(qry2[0:D, c, a, :].bitcast(f32), low[rows, s, 0, :].bitcast(f32)).then_inc(d_a[c], 16)

            def row_max(p, c):
                wait(sp, s_mr, p, NC, c)
                sp.dma_start(qry2[64:65, c, :, :].rearrange("o a t -> o (a t)")
                             .rearrange("o (r t) -> o r t", t=TB).bitcast(f32),
                             mrow[:, :].bitcast(f32)).then_inc(d_m, 16)

            def spread(p, c):
                wait(sp, s_lr, p, NC, c)
                wait(sp, s_rc, p, NC, c - 1)
                for a in range(2):
                    sp.dma_start(rcol[D * a:D * a + D, :], lrow[D * a:D * a + 1, :]
                                 .rearrange("o (r t) -> o r t", t=8)).then_inc(d_l, 16)
                wait(sp, s_rc, p, NC, c)
                wait(sp, d_b, p, NC, c - 1, 32)
                sp.dma_start(irow[:, :].rearrange("o (r t) -> o r t", t=8), icol[:, :]).then_inc(d_i, 16)
                wait(sp, d_i, p, NC, c, 16)
                wait(sp, s_yn, p, NC, c - 1)
                for a in range(2):
                    sp.dma_start(rb[D * a:D * a + D, :], irow[0:1, a * CH:(a + 1) * CH]
                                 .unsqueeze(1).to_broadcast([1, D, CH])).then_inc(d_b, 16)

            zero = Pair(0)
            operands(zero, 0)
            operands(zero, 1)
            row_max(zero, 0)
            operands(zero, 2)
            row_max(zero, 1)
            operands(zero, 3)

            def body(p):
                more = p.i is not None or p.n < PAIRS - 1
                nxt = p.ahead(1)
                if more:
                    wait(sp, s_wl, p, 1, 0)
                    first = 1 + p.n if p.i is None else p.i * 2 + (1 + p.n)
                    sp.dma_start(w_raw[:, :], w_qkv[bass.ds(first, 1), :, :].rearrange("o c n -> (o c) n"))\
                        .then_inc(d_w, 16)
                if p.n:
                    spread(p.ahead(-1), 3)
                row_max(p, 2)
                if more:
                    operands(nxt, 0)
                    wait(sp, s_op, p.ahead(-1), NC, NC - 1)
                    sp.dma_start(wo[:, nxt.parity(), :],
                                 w_o.rearrange("(n r) c -> n r c", r=128)[bass.ds(first, 1), :, :]
                                 .rearrange("o r c -> (o r) c")).then_inc(d_wo, 16)
                spread(p, 0)
                if more:
                    operands(nxt, 1)
                spread(p, 1)
                row_max(p, 3)
                if more:
                    operands(nxt, 2)
                    row_max(nxt, 0)
                spread(p, 2)
                if more:
                    row_max(nxt, 1)
                    operands(nxt, 3)

            over_pairs(nc, sp, body)
            spread(Pair(PAIRS - 1), NC - 1)
            for c in range(NC):
                sp.wait_ge(f_x, NC + c + 1)
                sp.dma_start(out_t[:, chunk(c)], x[:, chunk(c)]).then_inc(d_out, 16)
            sp.wait_ge(d_out, 16 * NC)

        @block.tensor
        def _(pe):
            def norm(k):
                for c in range(NC):
                    if k == 0:
                        pe.wait_ge(d_in[c], 16)
                    elif k == 1:
                        pe.wait_ge(f_x, c + 1)
                    else:
                        pe.wait_ge(s_xa, NC * (PAIRS - 1) + c + 1)
                    pe.matmul(ps[:, c, :], mean_w[:, :], x[:, chunk(c)], start=True, stop=True)\
                        .then_inc(l_mean, 1)
                for c in range(NC):
                    pe.wait_ge(l_sq, NC * k + c + 1)
                    for b in range(BPC):
                        t = BPC * c + b
                        mm = pe.matmul(ps[:, 4, t:t + 1], sq[:, t * TB:(t + 1) * TB], mean_w[:, 0:1],
                                       start=True, stop=True)
                    mm.then_inc(l_var, 1)
                pe.wait_ge(l_rs, k + 1)
                for c in range(NC):
                    for b in range(BPC):
                        t = BPC * c + b
                        for n, part_ in enumerate((rinvh, rinvl)):
                            mm = pe.matmul(ps[:, c, b * TB:(b + 1) * TB],
                                           part_[:, t:t + 1].to_broadcast([128, 128]), identr[:, :],
                                           start=n == 0, stop=n == 1)
                    mm.then_inc(l_sp, 1)

            def feed_forward(k):
                def values(c):
                    pe.wait_ge(f_ka, NC * k + c + 1)
                    pe.matmul(ps[:, c, :], wf[:, 2, :], aflat[:, (2 + c % 2) * CH:(3 + c % 2) * CH],
                              start=True, stop=True).then_inc(f_v, 1)

                for c in range(NC):
                    s = c % 2
                    base = (1 - s) * T
                    for n in range(2):
                        pe.wait_ge(f_mix, 2 * (NC * k + c) + n + 1)
                        if c >= 2:
                            pe.wait_ge((f_r, f_k)[n], NC * k + c - 1)
                        pe.matmul(ps[:, 4 + 2 * n + s, :], wf[:, n, :],
                                  pflat[:, base + (2 + n) * CH:base + (3 + n) * CH],
                                  start=True, stop=True).then_inc(f_z, 1)
                    if c:
                        values(c - 1)
                values(NC - 1)

            pe.wait_ge(s_set, 5)
            pe.wait_ge(d_c, 48)
            norm(0)
            feed_forward(0)
            norm(1)

            tasks = []

            def bank_free():
                if tasks:
                    kind, p, c, k = tasks.pop()
                    if kind == PROJ:
                        if k < 2:
                            wait(pe, s_lo, p, 8, 2 * c + k)
                        else:
                            wait(pe, s_hv, p, 12, 3 * c + 2)
                    else:
                        wait(pe, {MROW: s_mr, SUMS: s_lr, OUTP: s_xa}[kind], p, NC, c)

            def task(kind, p, c, k):
                bank_free()
                tasks.append((kind, p, c, k))
                if kind == PROJ:
                    if c == 0 and k == 0:
                        wait(pe, s_wl, p, 1, 0)
                    if k < 2:
                        for n, (w, xx) in enumerate(((wh, xh), (wl, xh), (wh, xl))):
                            mm = pe.matmul(misc[:, :], w[:, k * 128:(k + 1) * 128], xx[:, chunk(c)],
                                           start=n == 0, stop=n == 2)
                    else:
                        for b in range(BPC):
                            t = BPC * c + b
                            for n, (w, xx) in enumerate(((wh, xh), (wl, xh), (wh, xl))):
                                mm = pe.matmul(misc[:, b * TB:(b + 1) * TB], xx[:, t * TB:(t + 1) * TB],
                                               w[:, 256:384], start=n == 0, stop=n == 2)
                    mm.then_inc(s_pj, 1)
                elif kind == MROW:
                    wait(pe, s_nm, p, NC, c)
                    pe.transpose(misc[0:8, 0:128], neg[:, c % 2, :], ident[:, :]).then_inc(s_mt, 1)
                elif kind == SUMS:
                    wait(pe, s_ac, p, NU, LAST[c])
                    wait(pe, s_pa, p, NU, LAST[c])
                    for a in range(2):
                        mm = pe.matmul(misc[D * a:D * a + D, :], ones[:, :], part[:, c % 2, a, :],
                                       start=True, stop=True)
                    mm.then_inc(s_sum, 1)
                else:
                    wait(pe, s_yn, p, NC, c)
                    wait(pe, d_wo, p, 1, 0, 16)
                    pe.matmul(misc[:, :], wo[:, p.parity(), :], yn[:, :], start=True, stop=True)\
                        .then_inc(s_op, 1)

            def piece(p, g):
                c, b, a, k = PIECES[g]
                wait(pe, s_rd, p, NM, g - 2)
                if (b, a, k) == (0, 0, 0):
                    wait(pe, d_a[c], p, 1, 0, 192)
                if k == 0 and a == 0 and b == 0 and c == 0:
                    pass
                width = CH if k < c else (b + 1) * TB
                bank = ps[:, 5 + g % 2, :]
                mm = pe.matmul(bank[:, 0:width], qry1[:, c, a, b * TB:(b + 1) * TB],
                               keys1[:, p.parity(), k, a, 0:width], start=True, stop=k < c)
                if k == c:
                    mm = pe.matmul(bank[:, width - TB:width], identb[:, :], above[:, :],
                                   start=False, stop=True)
                mm.then_inc(s_mx, 1)

            def scores(p, u, a):
                c, j, off = UNITS[u]
                n = 2 * u + a
                if j == 0 and a == 0:
                    wait(pe, d_m, p, NC, c, 16)
                wait(pe, s_ex, p, 2 * NU, n - ST_RING if n >= ST_RING else n - 2)
                bank = ps[:, st_bank(n), :]
                blk = slice(j % BPC * TB, (j % BPC + 1) * TB)
                pe.matmul(bank[:, off:CH], keys1[:, p.parity(), j // BPC, a, blk],
                          qry1[:, c, a, off:CH], start=True, stop=False)
                pe.matmul(bank[:, off:CH], keys2[:, p.parity(), j // BPC, a, blk],
                          qry2[:, c, a, off:CH], start=False, stop=True).then_inc(s_st, 1)

            def weighted(p, u):
                c, j, off = UNITS[u]
                if j == 0:
                    wait(pe, s_yr, p, NC, c - 2)
                    wait(pe, s_hv, p, 12, 3 * c + 2)
                wait(pe, s_ex, p, 2 * NU, 2 * u + 1)
                if j >= BPC * c:
                    wait(pe, s_mk, p, NT, BPC * c + j % BPC)
                for a in range(2):
                    mm = pe.matmul(ps[D * a:D * a + D, 3 + c % 2, off:CH],
                                   vals[:, p.parity() * NT + j, D * a:D * a + D],
                                   prob[:, slot_of(u), a, off:CH],
                                   start=j == 0, stop=u == LAST[c])
                mm.then_inc(s_pv, 1)

            zero = Pair(0)
            pe.wait_ge(s_set, 6)
            for c in range(NC):
                pe.wait_ge(l_lo, c + 1)
            pe.wait_ge(l_hi, NC)
            for what, *rest in BEFORE:
                if what == "max":
                    for g in range(*rest):
                        piece(zero, g)
                else:
                    task(what, zero, rest[1], rest[2])

            def body(p):
                more = p.i is not None or p.n < PAIRS - 1
                for u in range(NU):
                    g = 2 * u + LEAD
                    ahead, g = (p, g) if g < NM else (p.ahead(1), g - NM)
                    lead = ahead is p or more
                    scores(p, u, 0)
                    if lead:
                        piece(ahead, g)
                    scores(p, u, 1)
                    if u:
                        weighted(p, u - 1)
                    elif p.n > 0:
                        weighted(p.ahead(-1), NU - 1)
                    if lead:
                        piece(ahead, g + 1)
                    if u in SIDE:
                        kind, k, c, n = SIDE[u]
                        if (k < 1 or more) and not (k < 0 and p.n == 0):
                            task(kind, p.ahead(k), c, n)
                if more:
                    tasks.clear()
                    kind, k, c, n = SIDE[SLOTS[-1]]
                    tasks.append((kind, p.ahead(k), c, n))

            over_pairs(nc, pe, body)
            last = Pair(PAIRS - 1)
            weighted(last, NU - 1)
            for kind in (SUMS, OUTP):
                task(kind, last, NC - 1, 0)
            norm(2)
            feed_forward(1)

        @block.scalar
        def _(act):
            def norm(k):
                for c in range(NC):
                    act.wait_ge(l_xc, NC * k + c + 1)
                    act.activation(sq[:, chunk(c)], xc[:, chunk(c)], ACT.Square).then_inc(l_sq, 1)
                act.wait_ge(l_var, NC * (k + 1))
                act.activation(rinv[:, :], ps[:, 4, 0:NT], ACT.Sqrt, bias=eps[:, 0:1]).then_inc(l_std, 1)

            def feed_forward(k):
                def nonlinear(c):
                    s = c % 2
                    act.wait_ge(f_z, 2 * (NC * k + c) + 1)
                    if c >= 2:
                        act.wait_ge(f_x, NC * k + c - 1)
                    act.activation(aflat[:, s * CH:(s + 1) * CH], ps[:, 4 + s, :], ACT.Sigmoid)\
                        .then_inc(f_r, 1)
                    act.wait_ge(f_z, 2 * (NC * k + c) + 2)
                    if c >= 2:
                        act.wait_ge(f_v, NC * k + c - 1)
                    if NC * k + c:
                        act.wait_ge(f_ka, NC * k + c)
                    act.activation(rb[:, :], ps[:, 6 + s, :], ACT.Relu).then_inc(f_k, 1)
                    act.wait_ge(f_k, NC * k + c + 1)
                    act.activation(aflat[:, (2 + s) * CH:(3 + s) * CH], rb[:, :], ACT.Square)\
                        .then_inc(f_ka, 1)

                for c in range(NC):
                    base = (1 - c % 2) * T
                    act.wait_ge(l_xn, NC * (2 * k) + (c + 1 if c == 0 else NC))
                    if c >= 2:
                        act.wait_ge(f_mix, 2 * (NC * k + c - 1))
                        act.wait_ge(f_z, 2 * (NC * k + c - 1))
                    for n in range(2):
                        act.activation(pflat[:, base + n * CH:base + (n + 1) * CH],
                                       xn[:, c * CH:(c + 1) * CH], ACT.Copy, scale=omu[:, n:n + 1])\
                            .then_inc(f_t, 1)
                    if c:
                        nonlinear(c - 1)
                nonlinear(NC - 1)

            act.wait_ge(s_set, 5)
            act.wait_ge(s_omu, 1)
            norm(0)
            feed_forward(0)
            norm(1)
            for c in range(NC):
                act.wait_ge(l_xn, NC + c + 1)
                act.activation(xh[:, chunk(c)], xn[:, 1 + c * CH:1 + (c + 1) * CH], ACT.Copy)\
                    .then_inc(l_hi, 1)

            def split_weights(p):
                wait(act, d_w, p, 1, 0, 16)
                wait(act, s_pj, p.ahead(-1), 12, 11)
                act.activation(wh[:, :], w_raw[:, :], ACT.Copy).then_inc(s_wh, 1)

            def task(kind, p, c, k):
                if kind == PROJ:
                    wait(act, s_pj, p, 12, 3 * c + k)
                    if k < 2:
                        if k == 0:
                            if c >= 2:
                                wait(act, d_a[c - 2], p, 1, 0, 192)
                            else:
                                wait(act, d_a[c + 2], p.ahead(-1), 1, 0, 192)
                        act.activation(high[:, c % 2, k, :], misc[:, :], ACT.Copy).then_inc(s_hv, 1)
                    else:
                        wait(act, s_pv, p.ahead(-2), NU, NU - 1)
                        v0 = p.parity() * NT + BPC * c
                        act.activation(vals[:, v0:v0 + BPC, :].rearrange("p b c -> p (b c)"), misc[:, :],
                                       ACT.Copy).then_inc(s_hv, 1)
                elif kind == MROW:
                    wait(act, s_mt, p, NC, c)
                    wait(act, d_m, p, NC, c - 1, 16)
                    act.activation(mrow[:, :], misc[0:8, 0:128], ACT.Copy).then_inc(s_mr, 1)
                elif kind == SUMS:
                    wait(act, s_sum, p, NC, c)
                    wait(act, d_l, p, NC, c - 1, 32)
                    act.activation(lrow[:, :], misc[:, :], ACT.Copy).then_inc(s_lr, 1)
                    wait(act, s_pv, p, NU, LAST[c])
                    wait(act, s_yn, p, NC, c - 1)
                    act.activation(yraw[:, :], ps[:, 3 + c % 2, :], ACT.Copy).then_inc(s_yr, 1)

            zero = Pair(0)
            split_weights(zero)
            for what, *rest in BEFORE:
                if what != "max":
                    task(what, zero, rest[1], rest[2])

            def body(p):
                more = p.i is not None or p.n < PAIRS - 1
                for u in range(NU):
                    c, j, off = UNITS[u]
                    wait(act, s_pv, p, NU, u - NP)
                    wait(act, s_ac, p, NU, u - NP)
                    wait(act, s_pa, p, NU, u - NP)
                    for a in range(2):
                        wait(act, s_st, p, 2 * NU, 2 * u + a)
                        act.activation(prob[:, slot_of(u), a, off:CH], ps[:, st_bank(2 * u + a), off:CH],
                                       ACT.Exp, scale=SCALE).then_inc(s_ex, 1)
                    if u in SIDE:
                        kind, k, cc, n = SIDE[u]
                        if (k < 1 or more) and not (k < 0 and p.n == 0):
                            task(kind, p.ahead(k), cc, n)
                    if u == 4 and more:
                        split_weights(p.ahead(1))

            over_pairs(nc, act, body)
            task(SUMS, Pair(PAIRS - 1), NC - 1, 0)
            norm(2)
            feed_forward(1)

        @block.vector
        def _(dve):
            def norm(k):
                for c in range(NC):
                    if k == 1:
                        dve.wait_ge(f_x, c + 1)
                    if k == 2:
                        dve.wait_ge(s_xa, NC * (PAIRS - 1) + c + 1)
                    dve.wait_ge(l_mean, NC * k + c + 1)
                    dve.tensor_tensor(xc[:, chunk(c)], x[:, chunk(c)], ps[:, c, :], ALU.subtract)\
                        .then_inc(l_xc, 1)
                dve.wait_ge(l_std, k + 1)
                dve.reciprocal(rinv[:, :], rinv[:, :]).then_inc(s_ri, 1)
                reciprocals[0] += 1
                dve.wait_ge(s_ri, reciprocals[0])
                dve.tensor_copy(rinvh[:, :], rinv[:, :]).then_inc(l_t, 1)
                dve.wait_ge(l_t, k + 1)
                dve.tensor_tensor(rinvl[:, :], rinv[:, :], rinvh[:, :].bitcast(f32), ALU.subtract)\
                    .then_inc(l_rs, 1)
                for c in range(NC):
                    dve.wait_ge(l_xc, NC * k + c + 1)
                    dve.wait_ge(l_sp, NC * k + c + 1)
                    dve.tensor_tensor(xn[:, 1 + c * CH:1 + (c + 1) * CH], xc[:, chunk(c)], ps[:, c, :],
                                      ALU.mult).then_inc(l_xn, 1)

            reciprocals = [0]

            def feed_forward(k):
                def update(c):
                    s = c % 2
                    dve.wait_ge(f_v, NC * k + c + 1)
                    dve.wait_ge(f_r, NC * k + c + 1)
                    if NC * k + c:
                        dve.wait_ge(f_x, NC * k + c)
                    dve.tensor_tensor(yn[:, :], ps[:, c, :], aflat[:, s * CH:(s + 1) * CH], ALU.mult)\
                        .then_inc(l_t2, 1)
                    dve.wait_ge(l_t2, NC * k + c + 1)
                    dve.scalar_tensor_tensor(x[:, chunk(c)], yn[:, :], 0.5, x[:, chunk(c)], ALU.mult,
                                             ALU.add).then_inc(f_x, 1)

                for c in range(NC):
                    base = (1 - c % 2) * T
                    if c >= 2:
                        dve.wait_ge(f_z, 2 * (NC * k + c - 1))
                    dve.wait_ge(l_xn, NC * (2 * k) + c + 1)
                    for n in range(2):
                        dve.wait_ge(f_t, 2 * (NC * k + c) + n + 1)
                        dve.scalar_tensor_tensor(pflat[:, base + (2 + n) * CH:base + (3 + n) * CH],
                                                 xn[:, 1 + c * CH:1 + (c + 1) * CH], mu[:, n:n + 1],
                                                 pflat[:, base + n * CH:base + (n + 1) * CH],
                                                 ALU.mult, ALU.add).then_inc(f_mix, 1)
                    if c:
                        update(c - 1)
                update(NC - 1)

            dve.wait_ge(s_set, 5)
            dve.tensor_copy(identr[:, :], ident[:, :])
            dve.tensor_copy(identb[:, :], ident[:, :])
            dve.memset(vflat[:, T - 1:T], 0.0)
            dve.wait_ge(d_x, 32)
            dve.tensor_scalar(omu[:, :], mu[:, :], -1.0, 1.0, ALU.mult, ALU.add).then_inc(s_omu, 1)
            norm(0)
            feed_forward(0)
            norm(1)
            for c in range(NC):
                dve.wait_ge(l_hi, c + 1)
                dve.tensor_tensor(xl[:, chunk(c)], xn[:, 1 + c * CH:1 + (c + 1) * CH],
                                  xh[:, chunk(c)].bitcast(f32), ALU.subtract).then_inc(l_lo, 1)

            def split_weights(p):
                wait(dve, s_wh, p, 1, 0)
                wait(dve, s_pj, p.ahead(-1), 12, 11)
                dve.tensor_tensor(wl[:, :], w_raw[:, :], wh[:, :].bitcast(f32), ALU.subtract)\
                    .then_inc(s_wl, 1)

            def task(kind, p, c, k):
                if kind == PROJ and k < 2:
                    wait(dve, s_hv, p, 12, 3 * c + k)
                    if k == 0:
                        if c >= 2:
                            wait(dve, d_a[c - 2], p, 1, 0, 192)
                        else:
                            wait(dve, d_a[c + 2], p.ahead(-1), 1, 0, 192)
                    dve.tensor_tensor(low[:, c % 2, k, :], misc[:, :], high[:, c % 2, k, :].bitcast(f32),
                                      ALU.subtract).then_inc(s_lo, 1)
                elif kind == RECIP:
                    wait(dve, d_l, p, NC, c, 32)
                    wait(dve, d_i, p, NC, c - 1, 16)
                    dve.reciprocal(icol[:, :], rcol[:, :]).then_inc(s_rc, 1)
                elif kind == NORM:
                    wait(dve, d_b, p, NC, c, 32)
                    wait(dve, s_yr, p, NC, c)
                    wait(dve, s_op, p, NC, c - 1)
                    dve.tensor_tensor(yn[:, :], yraw[:, :], rb[:, :], ALU.mult).then_inc(s_yn, 1)
                elif kind == OUTP:
                    wait(dve, s_op, p, NC, c)
                    wait(dve, s_xa, p, NC, c - NC)
                    dve.tensor_tensor(x[:, chunk(c)], x[:, chunk(c)], misc[:, :], ALU.add).then_inc(s_xa, 1)

            def piece(p, g):
                c, b, a, k = PIECES[g]
                width = CH if k < c else (b + 1) * TB
                wait(dve, s_mx, p, NM, g)
                dve.tensor_reduce(most[:, c % 2, 4 * a + b, k:k + 1], ps[:, 5 + g % 2, 0:width], AX.X,
                                  ALU.max).then_inc(s_rd, 1)

            def maxima(p, c):
                wait(dve, s_rd, p, NM, max(g for g in range(NM) if PIECES[g][0] == c))
                wait(dve, s_mt, p, NC, c - 2)
                dve.tensor_reduce(neg[:, c % 2, :], most[:, c % 2, :, 0:c + 1], AX.X, ALU.max,
                                  negate=True).then_inc(s_nm, 1)

            def sums(p, u):
                c, j, off = UNITS[u]
                if j == 0 or u == LAST[c]:
                    return
                s, s0 = slot_of(u), slot_of(u - 1)
                wait(dve, s_ex, p, 2 * NU, 2 * u + 1)
                if j >= BPC * c:
                    wait(dve, s_mk, p, NT, BPC * c + j % BPC)
                if j == 1:
                    wait(dve, s_sum, p, NC, c - 2)
                    if off:
                        dve.tensor_copy(part[:, c % 2, :, 0:off], prob[:, s0, :, 0:off])
                    dve.tensor_tensor(part[:, c % 2, :, off:POOL_FROM], prob[:, s0, :, off:POOL_FROM],
                                      prob[:, s, :, off:POOL_FROM], ALU.add).then_inc(s_ac, 2)
                else:
                    wait(dve, s_ac, p, NU, u - 1)
                    dve.tensor_tensor(part[:, c % 2, :, off:POOL_FROM], part[:, c % 2, :, off:POOL_FROM],
                                      prob[:, s, :, off:POOL_FROM], ALU.add)\
                        .then_inc(s_ac, 2 if u == LAST[c] - 1 else 1)

            MAXIMA = {3: (0, 2), 19: (0, 3), 23: (1, 0), 31: (1, 1)}
            zero = Pair(0)
            split_weights(zero)
            for what, *rest in BEFORE:
                if what == "max":
                    for g in range(*rest):
                        piece(zero, g)
                    if rest[1] < LEAD:
                        maxima(zero, 0 if rest[1] == 8 else 1)
                else:
                    task(what, zero, rest[1], rest[2])

            def side(p, u, more):
                for steps in (SIDE, DVE_SIDE):
                    if u in steps:
                        kind, k, c, n = steps[u]
                        if (k < 1 or more) and not (k < 0 and p.n == 0):
                            task(kind, p.ahead(k), c, n)
                if u in MAXIMA:
                    k, c = MAXIMA[u]
                    if k < 1 or more:
                        maxima(p.ahead(k), c)
                if u == 4 and more:
                    split_weights(p.ahead(1))

            def body(p):
                more = p.i is not None or p.n < PAIRS - 1
                for u in range(NU):
                    g = 2 * u + LEAD
                    ahead, g = (p, g) if g < NM else (p.ahead(1), g - NM)
                    lead = ahead is p or more
                    if lead:
                        piece(ahead, g)
                    if u:
                        side(p, u - 1, more)
                        sums(p, u - 1)
                    if lead:
                        piece(ahead, g + 1)
                sums(p, NU - 1)
                side(p, NU - 1, more)

            over_pairs(nc, dve, body)
            last = Pair(PAIRS - 1)
            for kind in (RECIP, NORM, OUTP):
                task(kind, last, NC - 1, 0)
            dve.memset(vflat[:, T - 1:T], 0.0).then_inc(l_t3, 1)
            norm(2)
            feed_forward(1)

        @block.gpsimd
        def _(pool):
            pool.memset(ident[:, :], 0.0).then_inc(s_pool, 1)
            pool.memset(above[:, :], 0.0).then_inc(s_pool, 1)
            pool.memset(ones[:, :], 1.0).then_inc(s_set, 1)
            pool.memset(mean_w[:, :], 1.0 / C).then_inc(s_set, 1)
            pool.memset(eps[:, :], EPS).then_inc(s_set, 1)
            pool.wait_ge(s_pool, 2)
            pool.wait_ge(s_set, 1)
            pool.affine_select(out=ident[:, :], in_=ident[:, :], compare_op=ALU.not_equal, fill=1.0,
                               base=0, pattern=[[-1, 128]], channel_multiplier=1).then_inc(s_set, 1)
            pool.affine_select(out=above[:, :], in_=above[:, :], compare_op=ALU.is_ge, fill=-1e30,
                               base=0, pattern=[[-1, 128]], channel_multiplier=1).then_inc(s_set, 1)
            pool.wait_ge(s_set, 5)
            pool.memset(keys2[64:65, :, :, :, :].bitcast(f32), 1.0).then_inc(s_set, 1)
            pool.wait_ge(s_set, 6)

            def body(p):
                for u in range(NU):
                    c, j, off = UNITS[u]
                    s, s0 = slot_of(u), slot_of(u - 1)
                    lo = max(off, POOL_FROM)
                    if j >= BPC * c:
                        wait(pool, s_ex, p, 2 * NU, 2 * u + 1)
                        pool.tensor_tensor(gate[:, u:u + 1], ones[:, 0:1], ones[:, 0:1], ALU.add)
                        diag = prob[:, s, :, off:off + TB]
                        pool.affine_select(out=diag, in_=diag, compare_op=ALU.is_ge, fill=0.0, base=0,
                                           pattern=[[0, 2], [1, TB]], channel_multiplier=-1)\
                            .then_inc(s_mk, 1)
                    if j == 0:
                        continue
                    wait(pool, s_ex, p, 2 * NU, 2 * u + 1)
                    if j >= BPC * c:
                        wait(pool, s_mk, p, NT, BPC * c + j % BPC)
                    if j == 1:
                        wait(pool, s_sum, p, NC, c - 2)
                        pool.tensor_tensor(part[:, c % 2, :, lo:CH], prob[:, s0, :, lo:CH],
                                           prob[:, s, :, lo:CH], ALU.add).then_inc(s_pa, 2)
                    else:
                        wait(pool, s_pa, p, NU, u - 1)
                        pool.tensor_tensor(part[:, c % 2, :, lo:CH], part[:, c % 2, :, lo:CH],
                                           prob[:, s, :, lo:CH], ALU.add).then_inc(s_pa, 1)

            over_pairs(nc, pool, body)


def kernel(**inputs):
    import concourse.bacc as _bacc
    from concourse import mybir as _mybir
    from concourse.bass_utils import run_bass_kernel_spmd as _run

    def a(name):
        return np.asarray(inputs["L0_" + name])

    def pairs(w):
        return w.reshape(PAIRS, 2 * D, C).transpose(0, 2, 1)

    arrays = {
        "x_t": a("attn_x_q").reshape(T, C).T,
        "w_qkv": np.concatenate([pairs(a("attn_w_q")), pairs(a("attn_w_k")), pairs(a("attn_w_v"))], axis=2),
        "w_o": a("attn_w_o"),
        "w_r": a("ffn_W_r").T, "w_k": a("ffn_W_k").T, "w_v": a("ffn_W_v").T,
        "mu_r": a("ffn_mu_r").reshape(C, 1), "mu_k": a("ffn_mu_k").reshape(C, 1),
    }
    arrays = {k: np.ascontiguousarray(v) for k, v in arrays.items()}
    nc = _bacc.Bacc("TRN2", target_bir_lowering=False, num_devices=1)
    args = [nc.dram_tensor(k, v.shape, _mybir.dt.from_np(v.dtype), kind="ExternalInput").ap()
            for k, v in arrays.items()]
    args.append(nc.dram_tensor("out_t", (C, T), _mybir.dt.float32, kind="ExternalOutput").ap())
    nc.disable_value_cache = True
    macaron_kernel(nc, *args)
    r = _run(nc, [arrays], core_ids=[0])
    return np.ascontiguousarray(r.results[0]["out_t"].T).reshape(1, T, C)
```

```python
import numpy as np
import concourse.bass as bass
from concourse import mybir
from contextlib import ExitStack


C = 128
T = 2048
H = 16
D = 64
PAIRS = H // 2
CH = 512
NC = T // CH
TB = 128
BPC = CH // TB
NT = T // TB
EPS = 1e-5
SCALE = D ** -0.5
POOL_FROM = 320

UNITS = [(c, j, max(0, j - BPC * c) * TB) for c in range(NC) for j in range(BPC * (c + 1))]
NU = len(UNITS)
LAST = [UNITS.index((c, BPC * (c + 1) - 1, CH - TB)) for c in range(NC)]
PIECES = [(c, b, a, k) for c in range(NC) for b in range(BPC) for a in range(2) for k in range(c + 1)]
NM = len(PIECES)
LEAD = 42
NP = 4
ST_RING = 3
PROJ, MROW, SUMS, OUTP, RECIP, NORM = "proj", "mrow", "sums", "outp", "recip", "norm"

SIDE = {1: (SUMS, -1, 3, 0), 4: (MROW, 0, 2, 0), 5: (PROJ, 1, 0, 0), 7: (PROJ, 1, 0, 1),
        8: (OUTP, -1, 3, 0), 9: (SUMS, 0, 0, 0), 10: (PROJ, 1, 0, 2), 11: (PROJ, 1, 1, 0),
        13: (PROJ, 1, 1, 1), 14: (PROJ, 1, 1, 2), 15: (OUTP, 0, 0, 0), 16: (SUMS, 0, 1, 0),
        17: (PROJ, 1, 2, 0), 19: (PROJ, 1, 2, 1), 20: (MROW, 0, 3, 0), 21: (PROJ, 1, 2, 2),
        22: (OUTP, 0, 1, 0), 24: (MROW, 1, 0, 0), 25: (SUMS, 0, 2, 0), 31: (OUTP, 0, 2, 0),
        32: (MROW, 1, 1, 0), 33: (PROJ, 1, 3, 0), 35: (PROJ, 1, 3, 1), 36: (PROJ, 1, 3, 2)}
DVE_SIDE = {3: (RECIP, -1, 3, 0), 7: (NORM, -1, 3, 0), 11: (RECIP, 0, 0, 0), 14: (NORM, 0, 0, 0),
            18: (RECIP, 0, 1, 0), 21: (NORM, 0, 1, 0), 27: (RECIP, 0, 2, 0), 30: (NORM, 0, 2, 0)}
SLOTS = sorted(SIDE)

PE_START = [("mean", 0), ("mean", 1), ("mean", 2), ("mean", 3), ("var", 0), ("var", 1), ("spread", 0),
            ("var", 2), ("spread", 1), ("var", 3), ("spread", 2), ("spread", 3), ("mixed", 0),
            ("mixed", 1), ("value", 0), ("mixed", 2), ("value", 1), ("mean", 4), ("mixed", 3),
            ("value", 2), ("mean", 5), ("var", 4), ("value", 3), ("var", 5), ("spread", 4),
            ("mean", 6), ("spread", 5), ("var", 6), ("mean", 7), ("proj", 0, 0), ("spread", 6),
            ("var", 7), ("proj", 0, 1), ("spread", 7), ("proj", 0, 2), ("proj", 1, 0), ("proj", 1, 1),
            ("proj", 1, 2), ("proj", 2, 0), ("max", 0, 4), ("proj", 2, 1), ("max", 4, 8),
            ("proj", 2, 2), ("mrow", 0), ("max", 8, 12), ("proj", 3, 0), ("max", 12, 16),
            ("proj", 3, 1), ("max", 16, 24), ("proj", 3, 2), ("mrow", 1), ("max", 24, LEAD)]
ACT_START = [("square", 0), ("square", 1), ("square", 2), ("square", 3), ("deviation", 0),
             ("deviation", 1), ("deviation", 2), ("previous", 0), ("deviation", 3), ("previous", 1),
             ("weights",), ("nonlinear", 0), ("previous", 2), ("nonlinear", 1), ("previous", 3),
             ("nonlinear", 2), ("square", 4), ("nonlinear", 3), ("square", 5), ("deviation", 4),
             ("deviation", 5), ("high", 0), ("square", 6), ("high", 1), ("deviation", 6),
             ("square", 7), ("proj", 0, 0), ("deviation", 7), ("high", 2), ("proj", 0, 1),
             ("high", 3), ("proj", 0, 2), ("proj", 1, 0), ("proj", 1, 1), ("proj", 1, 2),
             ("proj", 2, 0), ("proj", 2, 1), ("proj", 2, 2), ("mrow", 0), ("proj", 3, 0),
             ("proj", 3, 1), ("proj", 3, 2), ("mrow", 1)]
DVE_START = [("center", 0), ("center", 1), ("center", 2), ("center", 3), ("inverse", 0),
             ("inverse", 1), ("scale", 0), ("inverse", 2), ("scale", 1), ("mix", 0), ("inverse", 3),
             ("scale", 2), ("mix", 1), ("scale", 3), ("weights",), ("mix", 2), ("update", 0),
             ("mix", 3), ("update", 1), ("center", 4), ("update", 2), ("center", 5), ("inverse", 4),
             ("update", 3), ("inverse", 5), ("scale", 4), ("center", 6), ("low", 0), ("scale", 5),
             ("inverse", 6), ("center", 7), ("low", 1), ("proj", 0, 0), ("scale", 6),
             ("inverse", 7), ("low", 2), ("proj", 0, 1), ("scale", 7), ("low", 3), ("proj", 1, 0),
             ("proj", 1, 1), ("proj", 2, 0), ("max", 0, 4), ("proj", 2, 1), ("max", 4, 8),
             ("neg", 0), ("max", 8, 12), ("proj", 3, 0), ("max", 12, 16), ("proj", 3, 1),
             ("max", 16, 24), ("neg", 1), ("max", 24, LEAD)]
END_FIRST = {0: 19, 1: 25, 2: 32}
PE_END = {0: ("mean",), 1: ("var",), 2: ("spread",), 4: ("mixed",), 5: ("value",)}
ACT_END = {1: ("deviation",), 4: ("gate",)}
DVE_END = {0: ("center", "square"), 1: ("inverse",), 2: ("scale", "previous", "mix"),
           4: ("relu2",), 5: ("update",)}


def end_steps(steps, u):
    return [(name, c) for c, u0 in END_FIRST.items() for name in steps.get(u - u0, ())]


class Pair:

    def __init__(self, n, i=None, eng=None, bases=None):
        self.n, self.i, self.eng, self.bases = n, i, eng, bases

    def ahead(self, k):
        return Pair(self.n + k, self.i, self.eng, self.bases)

    def parity(self):
        return self.n % 2

    def count(self, sem, per_pair, index, each=1):
        fixed = (per_pair * self.n + index + 1) * each
        if self.i is None:
            return fixed
        if sem.name not in self.bases:
            self.bases[sem.name] = self.eng.snap(self.i * (2 * per_pair * each))
        return self.bases[sem.name] + fixed


def wait(eng, sem, pair, per_pair, index, each=1):
    n = pair.count(sem, per_pair, index, each)
    if not (isinstance(n, int) and n <= 0):
        eng.wait_ge(sem, n)


def over_pairs(nc, eng, body):
    body(Pair(0))
    with eng.Fori(0, (PAIRS - 2) // 2) as i:
        bases = {}
        body(Pair(1, i, eng, bases))
        body(Pair(2, i, eng, bases))
    body(Pair(PAIRS - 1))


def macaron_kernel(nc, x_t, w_qkv, w_o, w_r, w_k, w_v, mu_r, mu_k, out_t):
    f32, f32r, bf16 = mybir.dt.float32, mybir.dt.float32r, mybir.dt.bfloat16
    ALU, ACT, AX = mybir.AluOpType, mybir.ActivationFunctionType, mybir.AxisListType

    ctx = ExitStack()
    with ctx:
        def sb(name, shape, dt=f32):
            return ctx.enter_context(nc.sbuf_tensor(name, shape, dt))

        def sem(name):
            return ctx.enter_context(nc.semaphore(name))

        x = sb("x", [C, T])
        xh = sb("xh", [C, T], f32r)
        xl = sb("xl", [C, T], f32r)
        keys1 = sb("keys1", [128, 2, NC, 2, CH], f32r)
        keys2 = sb("keys2", [65, 2, NC, 2, CH], f32r)
        qry1 = sb("qry1", [128, NC, 2, CH], f32r)
        qry2 = sb("qry2", [65, NC, 2, CH], f32r)
        vz = sb("vz", [128, 1 + 2 * NT * C])
        vals = vz[:, 1:].rearrange("p (s c) -> p s c", c=C)
        high = sb("high", [128, 2, 2, CH], f32r)
        low = sb("low", [128, 2, 2, CH], f32r)
        prob = sb("prob", [128, NP, 2, CH])
        part = sb("part", [128, 2, 2, CH])
        yn = sb("yn", [128, CH])
        lrow = sb("lrow", [128, CH])
        rcol = sb("rcol", [128, 8])
        icol = sb("icol", [128, 8])
        irow = sb("irow", [1, 2 * CH])
        yraw = sb("yraw", [128, CH])
        rb = sb("rb", [128, CH])
        w_raw = sb("w_raw", [C, 3 * 128])
        wh = sb("wh", [C, 3 * 128], f32r)
        wl = sb("wl", [C, 3 * 128], f32r)
        wo = sb("wo", [128, 2, C])
        most = sb("most", [128, 2, 8, NC])
        neg = sb("neg", [128, 2, 8])
        mrow = sb("mrow", [8, 128], f32r)
        rinv = sb("rinv", [128, 3 * NT])
        ident = sb("ident", [128, 128])
        identb = sb("identb", [128, 128], bf16)
        above = sb("above", [128, 128], bf16)
        ones = sb("ones", [128, D])
        mean_w = sb("mean_w", [128, 128])
        eps = sb("eps", [128, 1])
        gate = sb("gate", [128, NU])
        wf = sb("wf", [C, 3, C])
        mu = sb("mu", [C, 2])
        omu = sb("omu", [C, 2])
        pflat = prob[:, :, :, :].rearrange("p s a t -> p (s a t)")
        aflat = part[:, :, :, :].rearrange("p s a t -> p (s a t)")
        hflat = high[:, :, :, :].rearrange("p s a t -> p (s a t)").bitcast(f32)
        lflat = low[:, :, :, :].rearrange("p s a t -> p (s a t)").bitcast(f32)
        xn = vz[:, 0:1 + T]

        def piece_of(flat, n):
            return flat[:, n * CH:(n + 1) * CH]

        def xc(i):
            return piece_of(pflat, i % NC) if i < 2 * NC else piece_of(hflat, 0)

        def sq(i):
            return piece_of(pflat, 4 + i % 2) if i < 2 * NC else piece_of(hflat, 1)

        def mixed(i, n):
            if i >= NC:
                return piece_of(hflat, 2 + n)
            return piece_of(pflat, 6 + n) if i % 2 == 0 else (lrow, yraw)[n][:, :]

        def gate_of(i):
            return piece_of(aflat, i % 2) if i < NC else piece_of(lflat, 0)

        def act_of(i):
            return piece_of(aflat, 2 + i % 2) if i < NC else piece_of(lflat, 1)

        def gated(i):
            return yn[:, :] if i < NC else piece_of(lflat, 2)

        ps = ctx.enter_context(nc.psum_tensor("ps", [128, 8, CH], f32))
        misc = ps[:, 7, :]

        def norm_bank(i):
            return i % NC if i < 2 * NC else 5

        def mix_bank(i, n):
            return 4 + n if i < NC else 6 - n


        s_set = sem("s_set")
        d_x, d_c, d_w, d_wo, d_m, d_out = (sem(n) for n in ("d_x", "d_c", "d_w", "d_wo", "d_m", "d_out"))
        d_in = [sem(f"d_in{c}") for c in range(NC)]
        d_a = [sem(f"d_a{c}") for c in range(NC)]
        l_mean, l_xc, l_sq, l_var, l_std, l_rs, l_sp, l_xn = (
            sem(n) for n in ("l_mean", "l_xc", "l_sq", "l_var", "l_std", "l_rs", "l_sp", "l_xn"))
        l_hi, l_lo = sem("l_hi"), sem("l_lo")
        f_t, f_mix, f_z, f_r, f_ka, f_v, f_g, f_x, f_k = (
            sem(n) for n in ("f_t", "f_mix", "f_z", "f_r", "f_ka", "f_v", "f_g", "f_x", "f_k"))
        s_omu = sem("s_omu")
        s_st, s_mx, s_pv, s_pj, s_mt, s_sum, s_op = (
            sem(n) for n in ("s_st", "s_mx", "s_pv", "s_pj", "s_mt", "s_sum", "s_op"))
        s_ex, s_hv, s_mr, s_lr, s_yr, s_wh = (
            sem(n) for n in ("s_ex", "s_hv", "s_mr", "s_lr", "s_yr", "s_wh"))
        d_l, d_i, d_b = (sem(n) for n in ("d_l", "d_i", "d_b"))
        s_rd, s_nm, s_ac, s_lo, s_rc, s_yn, s_xa, s_wl = (
            sem(n) for n in ("s_rd", "s_nm", "s_ac", "s_lo", "s_rc", "s_yn", "s_xa", "s_wl"))
        s_mk, s_pa = sem("s_mk"), sem("s_pa")
        s_pool = sem("s_pool")

        block = ctx.enter_context(nc.Block())

        def chunk(c):
            return slice(c * CH, (c + 1) * CH)

        def slot_of(u):
            return u % NP

        def st_bank(tile):
            return tile % ST_RING

        @block.sync
        def _(sp):
            for c in range(NC):
                sp.dma_start(x[:, chunk(c)], x_t[:, chunk(c)]).then_inc(d_in[c], 16)
            sp.dma_start(wf[:, 0, :], w_r).then_inc(d_c, 16)
            sp.dma_start(wf[:, 1, :], w_k).then_inc(d_c, 16)
            sp.dma_start(wf[:, 2, :], w_v).then_inc(d_c, 16)
            sp.dma_start(mu[:, 0:1], mu_r).then_inc(d_x, 16)
            sp.dma_start(mu[:, 1:2], mu_k).then_inc(d_x, 16)
            sp.dma_start(w_raw[:, :], w_qkv[0]).then_inc(d_w, 16)
            sp.dma_start(wo[:, 0, :], w_o[0:128, :]).then_inc(d_wo, 16)

            def operands(p, c):
                s, par = c % 2, p.parity()
                wait(sp, s_hv, p, 12, 3 * c + 1)
                wait(sp, s_lo, p, 8, 2 * c + 1)
                wait(sp, s_st, p.ahead(-2), 2 * NU, 2 * NU - 1)
                for a in range(2):
                    rows = slice(D * a, D * a + D)
                    sp.dma_start(keys1[0:D, par, c, a, :].bitcast(f32), high[rows, s, 1, :].bitcast(f32)).then_inc(d_a[c], 16)
                    sp.dma_start(keys1[D:128, par, c, a, :].bitcast(f32), low[rows, s, 1, :].bitcast(f32)).then_inc(d_a[c], 16)
                    sp.dma_start(keys2[0:D, par, c, a, :].bitcast(f32), high[rows, s, 1, :].bitcast(f32)).then_inc(d_a[c], 16)
                wait(sp, s_st, p.ahead(-1), 2 * NU, 2 * LAST[c] + 1)
                for a in range(2):
                    rows = slice(D * a, D * a + D)
                    sp.dma_start(qry1[0:D, c, a, :].bitcast(f32), high[rows, s, 0, :].bitcast(f32)).then_inc(d_a[c], 16)
                    sp.dma_start(qry1[D:128, c, a, :].bitcast(f32), high[rows, s, 0, :].bitcast(f32)).then_inc(d_a[c], 16)
                    sp.dma_start(qry2[0:D, c, a, :].bitcast(f32), low[rows, s, 0, :].bitcast(f32)).then_inc(d_a[c], 16)

            def row_max(p, c):
                wait(sp, s_mr, p, NC, c)
                sp.dma_start(qry2[64:65, c, :, :].rearrange("o a t -> o (a t)")
                             .rearrange("o (r t) -> o r t", t=TB).bitcast(f32),
                             mrow[:, :].bitcast(f32)).then_inc(d_m, 16)

            def spread(p, c):
                wait(sp, s_lr, p, NC, c)
                wait(sp, s_rc, p, NC, c - 1)
                for a in range(2):
                    sp.dma_start(rcol[D * a:D * a + D, :], lrow[D * a:D * a + 1, :]
                                 .rearrange("o (r t) -> o r t", t=8)).then_inc(d_l, 16)
                wait(sp, s_rc, p, NC, c)
                wait(sp, d_b, p, NC, c - 1, 32)
                sp.dma_start(irow[:, :].rearrange("o (r t) -> o r t", t=8), icol[:, :]).then_inc(d_i, 16)
                wait(sp, d_i, p, NC, c, 16)
                wait(sp, s_yn, p, NC, c - 1)
                for a in range(2):
                    sp.dma_start(rb[D * a:D * a + D, :], irow[0:1, a * CH:(a + 1) * CH]
                                 .unsqueeze(1).to_broadcast([1, D, CH])).then_inc(d_b, 16)

            zero = Pair(0)
            operands(zero, 0)
            operands(zero, 1)
            row_max(zero, 0)
            operands(zero, 2)
            row_max(zero, 1)
            operands(zero, 3)

            def body(p):
                more = p.i is not None or p.n < PAIRS - 1
                nxt = p.ahead(1)
                if more:
                    wait(sp, s_wl, p, 1, 0)
                    first = 1 + p.n if p.i is None else p.i * 2 + (1 + p.n)
                    sp.dma_start(w_raw[:, :], w_qkv[bass.ds(first, 1), :, :].rearrange("o c n -> (o c) n"))\
                        .then_inc(d_w, 16)
                if p.n:
                    spread(p.ahead(-1), 3)
                row_max(p, 2)
                if more:
                    operands(nxt, 0)
                    wait(sp, s_op, p.ahead(-1), NC, NC - 1)
                    sp.dma_start(wo[:, nxt.parity(), :],
                                 w_o.rearrange("(n r) c -> n r c", r=128)[bass.ds(first, 1), :, :]
                                 .rearrange("o r c -> (o r) c")).then_inc(d_wo, 16)
                spread(p, 0)
                if more:
                    operands(nxt, 1)
                spread(p, 1)
                row_max(p, 3)
                if more:
                    operands(nxt, 2)
                    row_max(nxt, 0)
                spread(p, 2)
                if more:
                    row_max(nxt, 1)
                    operands(nxt, 3)

            over_pairs(nc, sp, body)
            for c in range(NC):
                sp.wait_ge(f_x, NC + c + 1)
                sp.dma_start(out_t[:, chunk(c)], x[:, chunk(c)]).then_inc(d_out, 16)
            sp.wait_ge(d_out, 16 * NC)

        @block.tensor
        def _(pe):
            def normal(step, i):
                c = i % NC
                if step == "mean":
                    if i < NC:
                        pe.wait_ge(d_in[c], 16)
                    elif i < 2 * NC:
                        pe.wait_ge(f_x, i - NC + 1)
                    else:
                        pe.wait_ge(s_xa, NC * (PAIRS - 1) + c + 1)
                        if i == 2 * NC:
                            pe.wait_ge(s_rd, NM * PAIRS)
                        else:
                            pe.wait_ge(f_x, i - NC)
                    pe.matmul(ps[:, norm_bank(i), :], mean_w[:, :], x[:, chunk(c)],
                              start=True, stop=True).then_inc(l_mean, 1)
                elif step == "var":
                    pe.wait_ge(l_sq, i + 1)
                    for b in range(BPC):
                        mm = pe.matmul(ps[:, norm_bank(i), b:b + 1], sq(i)[:, b * TB:(b + 1) * TB],
                                       mean_w[:, 0:1], start=True, stop=True)
                    mm.then_inc(l_var, 1)
                else:
                    pe.wait_ge(l_rs, i + 1)
                    for b in range(BPC):
                        t = BPC * i + b
                        mm = pe.matmul(ps[:, norm_bank(i), b * TB:(b + 1) * TB],
                                       rinv[:, t:t + 1].to_broadcast([128, 128]), ident[:, :],
                                       start=True, stop=True)
                    mm.then_inc(l_sp, 1)

            def feed_forward(step, i):
                if step == "mixed":
                    for n in range(2):
                        pe.wait_ge(f_mix, 2 * i + n + 1)
                        if 0 < i < NC:
                            pe.wait_ge((f_r, f_k)[n], i)
                        pe.matmul(ps[:, mix_bank(i, n), :], wf[:, n, :], mixed(i, n),
                                  start=True, stop=True).then_inc(f_z, 1)
                else:
                    pe.wait_ge(f_ka, i + 1)
                    if i >= NC:
                        pe.wait_ge(f_r, i + 1)
                    elif i:
                        pe.wait_ge(f_g, i)
                    pe.matmul(ps[:, 6, :], wf[:, 2, :], act_of(i), start=True, stop=True)\
                        .then_inc(f_v, 1)

            tasks = []

            def bank_free():
                if tasks:
                    kind, p, c, k = tasks.pop()
                    if kind == PROJ:
                        if k < 2:
                            wait(pe, s_lo, p, 8, 2 * c + k)
                        else:
                            wait(pe, s_hv, p, 12, 3 * c + 2)
                    else:
                        if kind == SUMS and p.n == PAIRS - 1 and c == NC - 1:
                            kind = RECIP
                        wait(pe, {MROW: s_mr, SUMS: s_lr, RECIP: s_rc, OUTP: s_xa}[kind], p, NC, c)

            def task(kind, p, c, k):
                bank_free()
                tasks.append((kind, p, c, k))
                if kind == PROJ:
                    if p.i is None and p.n == 0 and k == 0:
                        pe.wait_ge(l_hi, c + 1)
                        pe.wait_ge(l_lo, c + 1)
                    if c == 0 and k == 0:
                        wait(pe, s_wl, p, 1, 0)
                    if k < 2:
                        for n, (w, xx) in enumerate(((wh, xh), (wl, xh), (wh, xl))):
                            mm = pe.matmul(misc[:, :], w[:, k * 128:(k + 1) * 128], xx[:, chunk(c)],
                                           start=n == 0, stop=n == 2)
                    else:
                        for b in range(BPC):
                            t = BPC * c + b
                            for n, (w, xx) in enumerate(((wh, xh), (wl, xh), (wh, xl))):
                                mm = pe.matmul(misc[:, b * TB:(b + 1) * TB], xx[:, t * TB:(t + 1) * TB],
                                               w[:, 256:384], start=n == 0, stop=n == 2)
                    mm.then_inc(s_pj, 1)
                elif kind == MROW:
                    wait(pe, s_nm, p, NC, c)
                    pe.transpose(misc[0:8, 0:128], neg[:, c % 2, :], ident[:, :]).then_inc(s_mt, 1)
                elif kind == SUMS:
                    wait(pe, s_ac, p, NU, LAST[c])
                    wait(pe, s_pa, p, NU, LAST[c])
                    for a in range(2):
                        mm = pe.matmul(misc[D * a:D * a + D, :], ones[:, :], part[:, c % 2, a, :],
                                       start=True, stop=True)
                    mm.then_inc(s_sum, 1)
                else:
                    wait(pe, s_yn, p, NC, c)
                    wait(pe, d_wo, p, 1, 0, 16)
                    pe.matmul(misc[:, :], wo[:, p.parity(), :], yn[:, :], start=True, stop=True)\
                        .then_inc(s_op, 1)

            def piece(p, g):
                c, b, a, k = PIECES[g]
                wait(pe, s_rd, p, NM, g - 2)
                if (b, a, k) == (0, 0, 0):
                    wait(pe, d_a[c], p, 1, 0, 192)
                if k == 0 and a == 0 and b == 0 and c == 0:
                    pass
                width = CH if k < c else (b + 1) * TB
                bank = ps[:, 5 + g % 2, :]
                mm = pe.matmul(bank[:, 0:width], qry1[:, c, a, b * TB:(b + 1) * TB],
                               keys1[:, p.parity(), k, a, 0:width], start=True, stop=k < c)
                if k == c:
                    mm = pe.matmul(bank[:, width - TB:width], identb[:, :], above[:, :],
                                   start=False, stop=True)
                mm.then_inc(s_mx, 1)

            def scores(p, u, a):
                c, j, off = UNITS[u]
                n = 2 * u + a
                if j == 0 and a == 0:
                    wait(pe, d_m, p, NC, c, 16)
                wait(pe, s_ex, p, 2 * NU, n - ST_RING if n >= ST_RING else n - 2)
                bank = ps[:, st_bank(n), :]
                blk = slice(j % BPC * TB, (j % BPC + 1) * TB)
                pe.matmul(bank[:, off:CH], keys1[:, p.parity(), j // BPC, a, blk],
                          qry1[:, c, a, off:CH], start=True, stop=False)
                pe.matmul(bank[:, off:CH], keys2[:, p.parity(), j // BPC, a, blk],
                          qry2[:, c, a, off:CH], start=False, stop=True).then_inc(s_st, 1)

            def weighted(p, u):
                c, j, off = UNITS[u]
                if j == 0:
                    wait(pe, s_yr, p, NC, c - 2)
                    wait(pe, s_hv, p, 12, 3 * c + 2)
                wait(pe, s_ex, p, 2 * NU, 2 * u + 1)
                if j >= BPC * c:
                    wait(pe, s_mk, p, NT, BPC * c + j % BPC)
                for a in range(2):
                    mm = pe.matmul(ps[D * a:D * a + D, 3 + c % 2, off:CH],
                                   vals[:, p.parity() * NT + j, D * a:D * a + D],
                                   prob[:, slot_of(u), a, off:CH],
                                   start=j == 0, stop=u == LAST[c])
                mm.then_inc(s_pv, 1)

            zero = Pair(0)
            pe.wait_ge(s_set, 5)
            for what, *rest in PE_START:
                if what in ("mean", "var", "spread"):
                    normal(what, rest[0])
                elif what in ("mixed", "value"):
                    if rest[0] == 0 and what == "mixed":
                        pe.wait_ge(d_c, 48)
                    feed_forward(what, rest[0])
                elif what == "max":
                    if rest[0] == 0:
                        pe.wait_ge(f_x, NC)
                    for g in range(*rest):
                        piece(zero, g)
                elif what == "proj":
                    task(PROJ, zero, *rest)
                else:
                    task(MROW, zero, rest[0], 0)
            pe.wait_ge(s_set, 6)

            def end_step(step, c):
                if step in ("mixed", "value"):
                    feed_forward(step, NC + c)
                else:
                    normal(step, 2 * NC + c)

            def body(p):
                more = p.i is not None or p.n < PAIRS - 1
                for u in range(NU):
                    g = 2 * u + LEAD
                    ahead, g = (p, g) if g < NM else (p.ahead(1), g - NM)
                    lead = ahead is p or more
                    scores(p, u, 0)
                    if lead:
                        piece(ahead, g)
                    scores(p, u, 1)
                    if u:
                        weighted(p, u - 1)
                    elif p.n > 0:
                        weighted(p.ahead(-1), NU - 1)
                    if lead:
                        piece(ahead, g + 1)
                    if u in SIDE:
                        kind, k, c, n = SIDE[u]
                        if (k < 1 or more) and not (k < 0 and p.n == 0):
                            task(kind, p.ahead(k), c, n)
                    if not more:
                        for step, c in end_steps(PE_END, u):
                            end_step(step, c)
                if more:
                    tasks.clear()
                    kind, k, c, n = SIDE[SLOTS[-1]]
                    tasks.append((kind, p.ahead(k), c, n))

            over_pairs(nc, pe, body)
            last = Pair(PAIRS - 1)
            weighted(last, NU - 1)
            for kind in (SUMS, OUTP):
                task(kind, last, NC - 1, 0)
            for steps in PE_END.values():
                for step in steps:
                    end_step(step, NC - 1)

        @block.scalar
        def _(act):
            def step(what, i):
                c = i % NC
                if what == "square":
                    act.wait_ge(l_xc, i + 1)
                    if i >= 2:
                        act.wait_ge(l_var, i - 1)
                    act.activation(sq(i), xc(i), ACT.Square).then_inc(l_sq, 1)
                elif what == "deviation":
                    act.wait_ge(l_var, i + 1)
                    act.activation(rinv[:, BPC * i:BPC * (i + 1)], ps[:, norm_bank(i), 0:BPC], ACT.Sqrt,
                                   bias=eps[:, 0:1]).then_inc(l_std, 1)
                elif what == "high":
                    act.wait_ge(l_xn, NC + i + 1)
                    act.activation(xh[:, chunk(c)], xn[:, 1 + c * CH:1 + (c + 1) * CH], ACT.Copy)\
                        .then_inc(l_hi, 1)
                elif what == "previous":
                    act.wait_ge(s_omu, 1)
                    act.wait_ge(l_xn, i + 1)
                    if i >= 2:
                        act.wait_ge(f_z, 2 * (i - 1))
                    for n in range(2):
                        act.activation(mixed(i, n), xn[:, c * CH:(c + 1) * CH], ACT.Copy,
                                       scale=omu[:, n:n + 1]).then_inc(f_t, 1)
                elif what == "gate":
                    act.wait_ge(f_z, 2 * i + 1)
                    if i >= 2:
                        act.wait_ge(f_x, i - 1 if i < NC else i)
                    act.activation(gate_of(i), ps[:, mix_bank(i, 0), :], ACT.Tanh, scale=0.5)\
                        .then_inc(f_r, 1)
                else:
                    step("gate", i)
                    act.wait_ge(f_z, 2 * i + 2)
                    if i >= 2:
                        act.wait_ge(f_v, i - 1)
                    if i:
                        act.wait_ge(f_ka, i)
                    act.activation(rb[:, :], ps[:, mix_bank(i, 1), :], ACT.Relu).then_inc(f_k, 1)
                    act.wait_ge(f_k, i + 1)
                    act.activation(act_of(i), rb[:, :], ACT.Square).then_inc(f_ka, 1)

            def split_weights(p):
                wait(act, d_w, p, 1, 0, 16)
                wait(act, s_pj, p.ahead(-1), 12, 11)
                act.activation(wh[:, :], w_raw[:, :], ACT.Copy).then_inc(s_wh, 1)

            def task(kind, p, c, k):
                if kind == PROJ:
                    wait(act, s_pj, p, 12, 3 * c + k)
                    if k < 2:
                        if k == 0:
                            if c >= 2:
                                wait(act, d_a[c - 2], p, 1, 0, 192)
                            else:
                                wait(act, d_a[c + 2], p.ahead(-1), 1, 0, 192)
                        act.activation(high[:, c % 2, k, :], misc[:, :], ACT.Copy).then_inc(s_hv, 1)
                    else:
                        wait(act, s_pv, p.ahead(-2), NU, NU - 1)
                        v0 = p.parity() * NT + BPC * c
                        act.activation(vals[:, v0:v0 + BPC, :].rearrange("p b c -> p (b c)"), misc[:, :],
                                       ACT.Copy).then_inc(s_hv, 1)
                elif kind == MROW:
                    wait(act, s_mt, p, NC, c)
                    wait(act, d_m, p, NC, c - 1, 16)
                    act.activation(mrow[:, :], misc[0:8, 0:128], ACT.Copy).then_inc(s_mr, 1)
                elif kind == SUMS:
                    wait(act, s_sum, p, NC, c)
                    wait(act, d_l, p, NC, c - 1, 32)
                    act.activation(lrow[:, :], misc[:, :], ACT.Copy).then_inc(s_lr, 1)
                    wait(act, s_pv, p, NU, LAST[c])
                    wait(act, s_yn, p, NC, c - 1)
                    act.activation(yraw[:, :], ps[:, 3 + c % 2, :], ACT.Copy).then_inc(s_yr, 1)

            zero = Pair(0)
            act.wait_ge(s_set, 5)
            for what, *rest in ACT_START:
                if what == "weights":
                    split_weights(zero)
                elif what == "proj":
                    task(PROJ, zero, *rest)
                elif what == "mrow":
                    task(MROW, zero, rest[0], 0)
                else:
                    step(what, rest[0])

            def body(p):
                more = p.i is not None or p.n < PAIRS - 1
                for u in range(NU):
                    c, j, off = UNITS[u]
                    wait(act, s_pv, p, NU, u - NP)
                    wait(act, s_ac, p, NU, u - NP)
                    wait(act, s_pa, p, NU, u - NP)
                    for a in range(2):
                        wait(act, s_st, p, 2 * NU, 2 * u + a)
                        act.activation(prob[:, slot_of(u), a, off:CH], ps[:, st_bank(2 * u + a), off:CH],
                                       ACT.Exp, scale=SCALE).then_inc(s_ex, 1)
                    if u in SIDE:
                        kind, k, cc, n = SIDE[u]
                        if (k < 1 or more) and not (k < 0 and p.n == 0):
                            task(kind, p.ahead(k), cc, n)
                    if u == 4 and more:
                        split_weights(p.ahead(1))
                    if not more:
                        for what, c in end_steps(ACT_END, u):
                            step(what, (NC if what == "gate" else 2 * NC) + c)

            over_pairs(nc, act, body)
            step("deviation", 3 * NC - 1)
            step("gate", 2 * NC - 1)

        @block.vector
        def _(dve):
            def step(what, i):
                c = i % NC
                if what == "center":
                    if i >= NC:
                        if i < 2 * NC:
                            dve.wait_ge(f_x, i - NC + 1)
                        else:
                            dve.wait_ge(s_xa, NC * (PAIRS - 1) + c + 1)
                    dve.wait_ge(l_mean, i + 1)
                    dve.tensor_tensor(xc(i), x[:, chunk(c)], ps[:, norm_bank(i), :], ALU.subtract)\
                        .then_inc(l_xc, 1)
                elif what == "square":
                    dve.wait_ge(l_xc, i + 1)
                    dve.tensor_tensor(sq(i), xc(i), xc(i), ALU.mult).then_inc(l_sq, 1)
                elif what == "inverse":
                    dve.wait_ge(l_std, i + 1)
                    dve.reciprocal(rinv[:, BPC * i:BPC * (i + 1)], rinv[:, BPC * i:BPC * (i + 1)])\
                        .then_inc(l_rs, 1)
                elif what == "scale":
                    dve.wait_ge(l_xc, i + 1)
                    dve.wait_ge(l_sp, i + 1)
                    if NC <= i < 2 * NC - 1:
                        dve.wait_ge(f_t, 2 * (i - NC) + 4)
                    dve.tensor_tensor(xn[:, 1 + c * CH:1 + (c + 1) * CH], xc(i),
                                      ps[:, norm_bank(i), :], ALU.mult).then_inc(l_xn, 1)
                elif what == "low":
                    dve.wait_ge(l_hi, i + 1)
                    dve.tensor_tensor(xl[:, chunk(c)], xn[:, 1 + c * CH:1 + (c + 1) * CH],
                                      xh[:, chunk(c)].bitcast(f32), ALU.subtract).then_inc(l_lo, 1)
                elif what == "previous":
                    dve.wait_ge(l_xn, 2 * NC + c + 1)
                    for n in range(2):
                        dve.tensor_scalar(mixed(i, n), xn[:, c * CH:(c + 1) * CH], omu[:, n:n + 1],
                                          None, ALU.mult).then_inc(f_t, 1)
                elif what == "mix":
                    for n in range(2):
                        dve.wait_ge(f_t, 2 * i + n + 1)
                        dve.scalar_tensor_tensor(mixed(i, n), xn[:, 1 + c * CH:1 + (c + 1) * CH],
                                                 mu[:, n:n + 1], mixed(i, n), ALU.mult, ALU.add)\
                            .then_inc(f_mix, 1)
                elif what == "relu2":
                    dve.wait_ge(f_z, 2 * i + 2)
                    dve.tensor_scalar(piece_of(lflat, 3), ps[:, mix_bank(i, 1), :], 0.0, None, ALU.max)\
                        .then_inc(f_k, 1)
                    dve.wait_ge(f_k, i + 1)
                    dve.tensor_tensor(act_of(i), piece_of(lflat, 3), ps[:, mix_bank(i, 1), :],
                                      ALU.mult).then_inc(f_ka, 1)
                else:
                    dve.wait_ge(f_v, i + 1)
                    dve.wait_ge(f_r, i + 1)
                    if i:
                        dve.wait_ge(f_x, i)
                    dve.scalar_tensor_tensor(gated(i), gate_of(i), 1.0, ps[:, 6, :], ALU.add, ALU.mult)\
                        .then_inc(f_g, 1)
                    dve.wait_ge(f_g, i + 1)
                    dve.scalar_tensor_tensor(x[:, chunk(c)], gated(i), 0.25, x[:, chunk(c)], ALU.mult,
                                             ALU.add).then_inc(f_x, 1)

            def split_weights(p):
                wait(dve, s_wh, p, 1, 0)
                wait(dve, s_pj, p.ahead(-1), 12, 11)
                dve.tensor_tensor(wl[:, :], w_raw[:, :], wh[:, :].bitcast(f32), ALU.subtract)\
                    .then_inc(s_wl, 1)

            def task(kind, p, c, k):
                if kind == PROJ and k < 2:
                    wait(dve, s_hv, p, 12, 3 * c + k)
                    if k == 0:
                        if c >= 2:
                            wait(dve, d_a[c - 2], p, 1, 0, 192)
                        else:
                            wait(dve, d_a[c + 2], p.ahead(-1), 1, 0, 192)
                    dve.tensor_tensor(low[:, c % 2, k, :], misc[:, :], high[:, c % 2, k, :].bitcast(f32),
                                      ALU.subtract).then_inc(s_lo, 1)
                elif kind == RECIP:
                    wait(dve, d_l, p, NC, c, 32)
                    wait(dve, d_i, p, NC, c - 1, 16)
                    dve.reciprocal(icol[:, :], rcol[:, :]).then_inc(s_rc, 1)
                elif kind == NORM:
                    wait(dve, d_b, p, NC, c, 32)
                    wait(dve, s_yr, p, NC, c)
                    wait(dve, s_op, p, NC, c - 1)
                    dve.tensor_tensor(yn[:, :], yraw[:, :], rb[:, :], ALU.mult).then_inc(s_yn, 1)
                elif kind == OUTP:
                    wait(dve, s_op, p, NC, c)
                    wait(dve, s_xa, p, NC, c - NC)
                    dve.tensor_tensor(x[:, chunk(c)], x[:, chunk(c)], misc[:, :], ALU.add).then_inc(s_xa, 1)

            def piece(p, g):
                c, b, a, k = PIECES[g]
                width = CH if k < c else (b + 1) * TB
                wait(dve, s_mx, p, NM, g)
                dve.tensor_reduce(most[:, c % 2, 4 * a + b, k:k + 1], ps[:, 5 + g % 2, 0:width], AX.X,
                                  ALU.max).then_inc(s_rd, 1)

            def maxima(p, c):
                wait(dve, s_rd, p, NM, max(g for g in range(NM) if PIECES[g][0] == c))
                wait(dve, s_mt, p, NC, c - 2)
                dve.tensor_reduce(neg[:, c % 2, :], most[:, c % 2, :, 0:c + 1], AX.X, ALU.max,
                                  negate=True).then_inc(s_nm, 1)

            def sums(p, u):
                c, j, off = UNITS[u]
                if j == 0 or u == LAST[c]:
                    return
                s, s0 = slot_of(u), slot_of(u - 1)
                wait(dve, s_ex, p, 2 * NU, 2 * u + 1)
                if j >= BPC * c:
                    wait(dve, s_mk, p, NT, BPC * c + j % BPC)
                if j == 1:
                    wait(dve, s_sum, p, NC, c - 2)
                    if off:
                        dve.tensor_copy(part[:, c % 2, :, 0:off], prob[:, s0, :, 0:off])
                    dve.tensor_tensor(part[:, c % 2, :, off:POOL_FROM], prob[:, s0, :, off:POOL_FROM],
                                      prob[:, s, :, off:POOL_FROM], ALU.add).then_inc(s_ac, 2)
                else:
                    wait(dve, s_ac, p, NU, u - 1)
                    dve.tensor_tensor(part[:, c % 2, :, off:POOL_FROM], part[:, c % 2, :, off:POOL_FROM],
                                      prob[:, s, :, off:POOL_FROM], ALU.add)\
                        .then_inc(s_ac, 2 if u == LAST[c] - 1 else 1)

            MAXIMA = {3: (0, 2), 19: (0, 3), 23: (1, 0), 31: (1, 1)}
            zero = Pair(0)
            dve.memset(vz[:, 0:1], 0.0)
            dve.wait_ge(s_set, 5)
            dve.tensor_copy(identb[:, :], ident[:, :])
            for what, *rest in DVE_START:
                if what == "weights":
                    split_weights(zero)
                elif what == "max":
                    for g in range(*rest):
                        piece(zero, g)
                elif what == "neg":
                    maxima(zero, rest[0])
                elif what == "proj":
                    task(PROJ, zero, *rest)
                else:
                    step(what, rest[0])
                if (what, rest) == ("center", [NC - 1]):
                    dve.wait_ge(d_x, 32)
                    dve.tensor_scalar(omu[:, :], mu[:, :], -1.0, 1.0, ALU.mult, ALU.add)\
                        .then_inc(s_omu, 1)

            def end_step(what, c):
                norm = what in ("center", "square", "inverse", "scale")
                step(what, (2 * NC if norm else NC) + c)

            def side(p, u, more):
                for steps in (SIDE, DVE_SIDE):
                    if u in steps:
                        kind, k, c, n = steps[u]
                        if (k < 1 or more) and not (k < 0 and p.n == 0):
                            task(kind, p.ahead(k), c, n)
                if u in MAXIMA:
                    k, c = MAXIMA[u]
                    if k < 1 or more:
                        maxima(p.ahead(k), c)
                if u == 4 and more:
                    split_weights(p.ahead(1))
                if not more:
                    for what, c in end_steps(DVE_END, u):
                        end_step(what, c)

            def body(p):
                more = p.i is not None or p.n < PAIRS - 1
                for u in range(NU):
                    g = 2 * u + LEAD
                    ahead, g = (p, g) if g < NM else (p.ahead(1), g - NM)
                    lead = ahead is p or more
                    if lead:
                        piece(ahead, g)
                    if u:
                        side(p, u - 1, more)
                        sums(p, u - 1)
                    if lead:
                        piece(ahead, g + 1)
                sums(p, NU - 1)
                side(p, NU - 1, more)

            over_pairs(nc, dve, body)
            last = Pair(PAIRS - 1)
            c = NC - 1
            wait(dve, s_sum, last, NC, c)
            dve.reciprocal(rb[:, :], misc[:, :]).then_inc(s_rc, 1)
            wait(dve, s_rc, last, NC, c)
            wait(dve, s_pv, last, NU, NU - 1)
            wait(dve, s_op, last, NC, c - 1)
            dve.tensor_tensor(yn[:, :], ps[:, 3 + c % 2, :], rb[:, :], ALU.mult).then_inc(s_yn, 1)
            task(OUTP, last, c, 0)
            for steps in DVE_END.values():
                for what in steps:
                    end_step(what, c)

        @block.gpsimd
        def _(pool):
            pool.memset(ident[:, :], 0.0).then_inc(s_pool, 1)
            pool.memset(above[:, :], 0.0).then_inc(s_pool, 1)
            pool.memset(ones[:, :], 1.0).then_inc(s_set, 1)
            pool.memset(mean_w[:, :], 1.0 / C).then_inc(s_set, 1)
            pool.memset(eps[:, :], EPS).then_inc(s_set, 1)
            pool.wait_ge(s_pool, 2)
            pool.wait_ge(s_set, 1)
            pool.affine_select(out=ident[:, :], in_=ident[:, :], compare_op=ALU.not_equal, fill=1.0,
                               base=0, pattern=[[-1, 128]], channel_multiplier=1).then_inc(s_set, 1)
            pool.affine_select(out=above[:, :], in_=above[:, :], compare_op=ALU.is_ge, fill=-1e30,
                               base=0, pattern=[[-1, 128]], channel_multiplier=1).then_inc(s_set, 1)
            pool.wait_ge(s_set, 5)
            pool.memset(keys2[64:65, :, :, :, :].bitcast(f32), 1.0).then_inc(s_set, 1)
            pool.wait_ge(s_set, 6)

            def body(p):
                for u in range(NU):
                    c, j, off = UNITS[u]
                    s, s0 = slot_of(u), slot_of(u - 1)
                    lo = max(off, POOL_FROM)
                    if j >= BPC * c:
                        wait(pool, s_ex, p, 2 * NU, 2 * u + 1)
                        pool.tensor_tensor(gate[:, u:u + 1], ones[:, 0:1], ones[:, 0:1], ALU.add)
                        diag = prob[:, s, :, off:off + TB]
                        pool.affine_select(out=diag, in_=diag, compare_op=ALU.is_ge, fill=0.0, base=0,
                                           pattern=[[0, 2], [1, TB]], channel_multiplier=-1)\
                            .then_inc(s_mk, 1)
                    if j == 0:
                        continue
                    wait(pool, s_ex, p, 2 * NU, 2 * u + 1)
                    if j >= BPC * c:
                        wait(pool, s_mk, p, NT, BPC * c + j % BPC)
                    if j == 1:
                        wait(pool, s_sum, p, NC, c - 2)
                        pool.tensor_tensor(part[:, c % 2, :, lo:CH], prob[:, s0, :, lo:CH],
                                           prob[:, s, :, lo:CH], ALU.add).then_inc(s_pa, 2)
                    else:
                        wait(pool, s_pa, p, NU, u - 1)
                        pool.tensor_tensor(part[:, c % 2, :, lo:CH], part[:, c % 2, :, lo:CH],
                                           prob[:, s, :, lo:CH], ALU.add).then_inc(s_pa, 1)

            over_pairs(nc, pool, body)


def kernel(**inputs):
    import concourse.bacc as _bacc
    from concourse import mybir as _mybir
    from concourse.bass_utils import run_bass_kernel_spmd as _run

    def a(name):
        return np.asarray(inputs["L0_" + name])

    def pairs(w):
        return w.reshape(PAIRS, 2 * D, C).transpose(0, 2, 1)

    arrays = {
        "x_t": a("attn_x_q").reshape(T, C).T,
        "w_qkv": np.concatenate([pairs(a("attn_w_q")), pairs(a("attn_w_k")), pairs(a("attn_w_v"))], axis=2),
        "w_o": a("attn_w_o"),
        "w_r": a("ffn_W_r").T, "w_k": a("ffn_W_k").T, "w_v": a("ffn_W_v").T,
        "mu_r": a("ffn_mu_r").reshape(C, 1), "mu_k": a("ffn_mu_k").reshape(C, 1),
    }
    arrays = {k: np.ascontiguousarray(v) for k, v in arrays.items()}
    nc = _bacc.Bacc("TRN2", target_bir_lowering=False, num_devices=1)
    args = [nc.dram_tensor(k, v.shape, _mybir.dt.from_np(v.dtype), kind="ExternalInput").ap()
            for k, v in arrays.items()]
    args.append(nc.dram_tensor("out_t", (C, T), _mybir.dt.float32, kind="ExternalOutput").ap())
    nc.disable_value_cache = True
    macaron_kernel(nc, *args)
    r = _run(nc, [arrays], core_ids=[0])
    return np.ascontiguousarray(r.results[0]["out_t"].T).reshape(1, T, C)
```

```python
import numpy as np
import concourse.bass as bass
from concourse import mybir
from contextlib import ExitStack


C = 128
T = 2048
H = 16
D = 64
PAIRS = H // 2
CH = 512
NC = T // CH
TB = 128
BPC = CH // TB
NT = T // TB
EPS = 1e-5
SCALE = D ** -0.5
POOL_FROM = 288

UNITS = [(c, j, max(0, j - BPC * c) * TB) for c in range(NC) for j in range(BPC * (c + 1))]
NU = len(UNITS)
LAST = [UNITS.index((c, BPC * (c + 1) - 1, CH - TB)) for c in range(NC)]
PIECES = [(c, b, a, k) for c in range(NC) for b in range(BPC) for a in range(2) for k in range(c + 1)]
NM = len(PIECES)
LEAD = 42
NP = 4
ST_RING = 3
KH, KL, QH, QL = range(4)
PROJ, MROW, SUMS, OUTP, RECIP, NORM = "proj", "mrow", "sums", "outp", "recip", "norm"

SIDE = {1: (SUMS, -1, 3, 0), 4: (MROW, 0, 2, 0), 5: (PROJ, 1, 0, 0), 7: (PROJ, 1, 0, 1),
        8: (SUMS, 0, 0, 0), 9: (OUTP, -1, 3, 0), 10: (PROJ, 1, 0, 2), 11: (PROJ, 1, 1, 0),
        13: (PROJ, 1, 1, 1), 14: (PROJ, 1, 1, 2), 15: (OUTP, 0, 0, 0), 16: (SUMS, 0, 1, 0),
        17: (PROJ, 1, 2, 0), 19: (PROJ, 1, 2, 1), 20: (MROW, 0, 3, 0), 21: (PROJ, 1, 2, 2),
        22: (OUTP, 0, 1, 0), 24: (MROW, 1, 0, 0), 25: (SUMS, 0, 2, 0), 31: (OUTP, 0, 2, 0),
        32: (MROW, 1, 1, 0), 33: (PROJ, 1, 3, 0), 35: (PROJ, 1, 3, 1), 37: (PROJ, 1, 3, 2)}
DVE_SIDE = {3: (RECIP, -1, 3, 0), 7: (NORM, -1, 3, 0), 10: (RECIP, 0, 0, 0), 13: (NORM, 0, 0, 0),
            17: (RECIP, 0, 1, 0), 20: (NORM, 0, 1, 0), 26: (RECIP, 0, 2, 0), 29: (NORM, 0, 2, 0)}
MAXIMA = {3: (2, 0), 19: (3, 0), 23: (0, 1), 30: (1, 1)}
LEAD_0 = 24
SIDE_0 = {u: s for u, s in SIDE.items() if s[1] >= 0 and s[:3] != (MROW, 0, 2)}
SIDE_0.update({0: (MROW, 0, 1, 0), 1: (PROJ, 0, 3, 0), 2: (PROJ, 0, 3, 1), 3: (PROJ, 0, 3, 2),
               9: (MROW, 0, 2, 0)})
MAXIMA_0 = {7: (2, 0), 19: (3, 0), 23: (0, 1), 30: (1, 1)}


def slots_of(p, steps, first=None):
    if p.i is None and p.n == 0:
        return first or {u: s for u, s in steps.items() if s[1] >= 0}
    if p.i is None:
        return {u: s for u, s in steps.items() if s[1] < 1}
    return steps


def pieces_in(p, u):
    def before(u):
        return min(LEAD_0 + 3 * u, LEAD + 2 * u) if p.i is None and p.n == 0 else LEAD + 2 * u
    return [(p, g) if g < NM else (p.ahead(1), g - NM) for g in range(before(u), before(u + 1))
            if g < NM or p.i is not None or p.n == 0]



PE_START = [("mean", 0), ("mean", 1), ("mean", 2), ("mean", 3), ("var", 0), ("var", 1), ("spread", 0),
            ("var", 2), ("spread", 1), ("var", 3), ("spread", 2), ("spread", 3), ("mixed", 0),
            ("mixed", 1), ("value", 0), ("mixed", 2), ("value", 1), ("mean", 4), ("mixed", 3),
            ("value", 2), ("mean", 5), ("var", 4), ("value", 3), ("spread", 4), ("var", 5),
            ("mean", 6), ("spread", 5), ("proj", 0, 0), ("var", 6), ("mean", 7), ("proj", 0, 1),
            ("spread", 6), ("var", 7), ("spread", 7), ("proj", 0, 2), ("proj", 1, 0), ("proj", 1, 1),
            ("proj", 1, 2), ("proj", 2, 0), ("max", 0, 4), ("proj", 2, 1), ("max", 4, 8),
            ("proj", 2, 2), ("max", 8, 12), ("mrow", 0), ("max", 12, 24)]
ACT_START = [("square", 0), ("square", 1), ("square", 2), ("square", 3), ("deviation", 0),
             ("deviation", 1), ("deviation", 2), ("previous", 0), ("deviation", 3), ("previous", 1),
             ("weights",), ("nonlinear", 0), ("previous", 2), ("nonlinear", 1), ("previous", 3),
             ("nonlinear", 2), ("square", 4), ("nonlinear", 3), ("deviation", 4), ("square", 5),
             ("high", 0), ("deviation", 5), ("square", 6), ("proj", 0, 0), ("deviation", 6),
             ("high", 1), ("square", 7), ("proj", 0, 1), ("deviation", 7), ("high", 2),
             ("high", 3), ("proj", 0, 2), ("proj", 1, 0), ("proj", 1, 1), ("proj", 1, 2),
             ("proj", 2, 0), ("proj", 2, 1), ("proj", 2, 2), ("mrow", 0)]
DVE_START = [("center", 0), ("center", 1), ("center", 2), ("center", 3), ("inverse", 0),
             ("inverse", 1), ("scale", 0), ("inverse", 2), ("scale", 1), ("mix", 0), ("inverse", 3),
             ("scale", 2), ("mix", 1), ("scale", 3), ("weights",), ("mix", 2), ("update", 0),
             ("mix", 3), ("update", 1), ("center", 4), ("update", 2), ("center", 5), ("inverse", 4),
             ("update", 3), ("scale", 4), ("inverse", 5), ("center", 6), ("low", 0), ("scale", 5),
             ("inverse", 6), ("proj", 0, 0), ("center", 7), ("low", 1), ("proj", 0, 1), ("scale", 6),
             ("inverse", 7), ("scale", 7), ("low", 2), ("low", 3), ("proj", 1, 0),
             ("proj", 1, 1), ("proj", 2, 0), ("max", 0, 4), ("proj", 2, 1), ("max", 4, 8),
             ("neg", 0), ("max", 8, 24), ("neg", 1)]
HALF = CH // 2
PE_LAST = [("mean", 0), ("mean", 1), ("var", 0), ("var", 1), ("spread", 0), ("spread", 1),
           ("mixed", 0), ("mixed", 1), ("value", 0), ("value", 1)]
ACT_LAST = [("square", 0), ("square", 1), ("deviation", 0), ("deviation", 1), ("previous", 0),
            ("previous", 1), ("nonlinear", 0), ("nonlinear", 1)]
DVE_LAST = [("center", 0), ("center", 1), ("inverse", 0), ("inverse", 1), ("scale", 0), ("scale", 1),
            ("mix", 0), ("mix", 1), ("update", 0), ("update", 1)]
END_FIRST = {0: 19, 1: 25, 2: 33}
PE_END = {0: ("mean",), 1: ("var",), 2: ("spread",), 4: ("mixed",), 5: ("value",)}
ACT_END = {1: ("deviation",), 4: ("gate",)}
DVE_END = {0: ("center", "square"), 1: ("inverse",), 2: ("scale", "previous", "mix"),
           4: ("relu2",), 5: ("update",)}


def end_steps(steps, u):
    return [(name, c) for c, u0 in END_FIRST.items() for name in steps.get(u - u0, ())]


class Pair:

    def __init__(self, n, i=None, eng=None, bases=None):
        self.n, self.i, self.eng, self.bases = n, i, eng, bases

    def ahead(self, k):
        return Pair(self.n + k, self.i, self.eng, self.bases)

    def parity(self):
        return self.n % 2

    def count(self, sem, per_pair, index, each=1):
        fixed = (per_pair * self.n + index + 1) * each
        if self.i is None:
            return fixed
        if sem.name not in self.bases:
            self.bases[sem.name] = self.eng.snap(self.i * (2 * per_pair * each))
        return self.bases[sem.name] + fixed


def wait(eng, sem, pair, per_pair, index, each=1):
    n = pair.count(sem, per_pair, index, each)
    if not (isinstance(n, int) and n <= 0):
        eng.wait_ge(sem, n)


def over_pairs(nc, eng, body):
    body(Pair(0))
    with eng.Fori(0, (PAIRS - 2) // 2) as i:
        bases = {}
        body(Pair(1, i, eng, bases))
        body(Pair(2, i, eng, bases))
    body(Pair(PAIRS - 1))


def macaron_kernel(nc, x_t, w_qkv, w_o, w_r, w_k, w_v, mu_r, mu_k, out_t):
    f32, f32r, bf16 = mybir.dt.float32, mybir.dt.float32r, mybir.dt.bfloat16
    ALU, ACT, AX = mybir.AluOpType, mybir.ActivationFunctionType, mybir.AxisListType

    ctx = ExitStack()
    with ctx:
        def sb(name, shape, dt=f32):
            return ctx.enter_context(nc.sbuf_tensor(name, shape, dt))

        def sem(name):
            return ctx.enter_context(nc.semaphore(name))

        x = sb("x", [C, T])
        xh = sb("xh", [C, T], f32r)
        xl = sb("xl", [C, T], f32r)
        terms1 = sb("terms1", [128, 3 * NC, 2, CH], f32r)
        terms2 = sb("terms2", [65, 3 * NC, 2, CH], f32r)
        vz = sb("vz", [128, 1 + 2 * NT * C])
        vals = vz[:, 1:].rearrange("p (s c) -> p s c", c=C)
        split = sb("split", [128, 2, 4, CH], f32r)
        prob = sb("prob", [128, NP, 2, CH])
        part = sb("part", [128, 2, 2, CH])
        yn = sb("yn", [128, CH])
        lrow = sb("lrow", [128, CH])
        rcol = sb("rcol", [128, 8])
        icol = sb("icol", [128, 8])
        irow = sb("irow", [1, 2 * CH])
        yraw = sb("yraw", [128, CH])
        rb = sb("rb", [128, CH])
        w_raw = sb("w_raw", [C, 3 * 128])
        wh = sb("wh", [C, 3 * 128], f32r)
        wl = sb("wl", [C, 3 * 128], f32r)
        wo = sb("wo", [128, 2, C])
        most = sb("most", [128, 2, 8, NC])
        neg = sb("neg", [128, 2, 8])
        mrow = sb("mrow", [8, 128], f32r)
        rinv = sb("rinv", [128, 3 * NT + BPC])
        ident = sb("ident", [128, 128])
        identb = sb("identb", [128, 128], bf16)
        above = sb("above", [128, 128], bf16)
        ones = sb("ones", [128, D])
        mean_w = sb("mean_w", [128, 128])
        eps = sb("eps", [128, 1])
        gate = sb("gate", [128, NU])
        warm = sb("warm", [128, 3])
        wf = sb("wf", [C, 3, C])
        mu = sb("mu", [C, 2])
        omu = sb("omu", [C, 2])
        pflat = prob[:, :, :, :].rearrange("p s a t -> p (s a t)")
        aflat = part[:, :, :, :].rearrange("p s a t -> p (s a t)")
        sflat = split[:, :, :, :].rearrange("p s a t -> p (s a t)").bitcast(f32)
        hflat, lflat = sflat[:, 0:T], sflat[:, T:2 * T]
        xn = vz[:, 0:1 + T]

        def piece_of(flat, n):
            return flat[:, n * CH:(n + 1) * CH]

        def span(i):
            if i < 3 * NC - 1:
                return chunk(i % NC), slice(0, CH)
            h = i - (3 * NC - 1)
            return (slice((NC - 1) * CH + h * HALF, (NC - 1) * CH + (h + 1) * HALF),
                    slice(h * HALF, (h + 1) * HALF))

        def norm_of(i):
            return i if i < NC else i + NC

        def xc(i):
            return piece_of(pflat, i % NC) if i < 2 * NC else piece_of(hflat, 0)

        def sq(i):
            return piece_of(pflat, 4 + i % 2) if i < 2 * NC else piece_of(hflat, 1)

        def mixed(i, n):
            if i >= NC:
                return piece_of(hflat, 2 + n)
            return piece_of(pflat, 6 + n) if i % 2 == 0 else (lrow, yraw)[n][:, :]

        def gate_of(i):
            return piece_of(aflat, i % 2) if i < NC else piece_of(lflat, 0)

        def act_of(i):
            return piece_of(aflat, 2 + i % 2) if i < NC else piece_of(lflat, 1)

        def relu_of(i):
            return rb[:, :] if i < NC else piece_of(lflat, 3)

        def gated(i):
            return yn[:, :] if i < NC else piece_of(lflat, 2)

        ps = ctx.enter_context(nc.psum_tensor("ps", [128, 8, CH], f32))
        misc = ps[:, 7, :]

        def bank_of(kind, p, c, k):
            early = kind == PROJ and p.i is None and p.n == 0 and c < NC - 1
            return ps[:, 4, :] if early and (3 * c + k) % 2 else misc

        def max_bank(p, g):
            early = p.i is None and p.n == 0 and g < LEAD_0
            return ((5, 6, 0, 1)[g % 4], 4) if early else (5 + g % 2, 2)

        def norm_bank(i):
            return i % NC if i < 2 * NC else 5 if i < 3 * NC else 0

        def mix_bank(i, n):
            return 4 + n if i < NC else 6 - n if i < 2 * NC else 1 - n

        def value_bank(i):
            return 6 if i < 2 * NC else 1


        s_set = sem("s_set")
        d_x, d_c, d_w, d_wo, d_m, d_out = (sem(n) for n in ("d_x", "d_c", "d_w", "d_wo", "d_m", "d_out"))
        d_in = [sem(f"d_in{c}") for c in range(NC)]
        d_a = [sem(f"d_a{c}") for c in range(NC)]
        l_mean, l_xc, l_sq, l_var, l_std, l_rs, l_sp, l_xn = (
            sem(n) for n in ("l_mean", "l_xc", "l_sq", "l_var", "l_std", "l_rs", "l_sp", "l_xn"))
        l_hi, l_lo = sem("l_hi"), sem("l_lo")
        f_t, f_mix, f_z, f_r, f_ka, f_v, f_g, f_x, f_k = (
            sem(n) for n in ("f_t", "f_mix", "f_z", "f_r", "f_ka", "f_v", "f_g", "f_x", "f_k"))
        s_omu = sem("s_omu")
        s_st, s_mx, s_pv, s_pj, s_mt, s_sum, s_op = (
            sem(n) for n in ("s_st", "s_mx", "s_pv", "s_pj", "s_mt", "s_sum", "s_op"))
        s_ex, s_hv, s_mr, s_lr, s_yr, s_wh = (
            sem(n) for n in ("s_ex", "s_hv", "s_mr", "s_lr", "s_yr", "s_wh"))
        d_l, d_i, d_b = (sem(n) for n in ("d_l", "d_i", "d_b"))
        s_rd, s_nm, s_ac, s_lo, s_rc, s_yn, s_xa, s_wl = (
            sem(n) for n in ("s_rd", "s_nm", "s_ac", "s_lo", "s_rc", "s_yn", "s_xa", "s_wl"))
        s_mk, s_pa = sem("s_mk"), sem("s_pa")
        s_pool = sem("s_pool")

        block = ctx.enter_context(nc.Block())

        def chunk(c):
            return slice(c * CH, (c + 1) * CH)

        def slot_of(u):
            return u % NP

        def st_bank(tile):
            return tile % ST_RING

        @block.sync
        def _(sp):
            for c in range(NC):
                sp.dma_start(x[:, chunk(c)], x_t[:, chunk(c)]).then_inc(d_in[c], 16)
            sp.dma_start(wf[:, 0, :], w_r).then_inc(d_c, 16)
            sp.dma_start(wf[:, 1, :], w_k).then_inc(d_c, 16)
            sp.dma_start(wf[:, 2, :], w_v).then_inc(d_c, 16)
            sp.dma_start(mu[:, 0:1], mu_r).then_inc(d_x, 16)
            sp.dma_start(mu[:, 1:2], mu_k).then_inc(d_x, 16)
            sp.dma_start(w_raw[:, :], w_qkv[0]).then_inc(d_w, 16)
            sp.dma_start(wo[:, 0, :], w_o[0:128, :]).then_inc(d_wo, 16)

            def operands(p, c):
                s, par = c % 2, p.parity()
                wait(sp, s_hv, p, 12, 3 * c + 1)
                wait(sp, s_lo, p, 8, 2 * c + 1)
                wait(sp, s_st, p.ahead(-2), 2 * NU, 2 * NU - 1)
                wait(sp, s_st, p.ahead(-1), 2 * NU, 2 * LAST[c] + 1)
                key, query = par * NC + c, 2 * NC + c
                both = slice(key, query + 1, query - key)
                for a in range(2):
                    rows = slice(D * a, D * a + D)
                    for to, k_from, q_from in ((terms1[0:D], KH, QH), (terms1[D:128], KL, QH),
                                               (terms2[0:D], KH, QL)):
                        sp.dma_start(to[:, both, a, :].bitcast(f32),
                                     split[rows, s, k_from:q_from + 1:q_from - k_from, :].bitcast(f32))\
                            .then_inc(d_a[c], 16)

            def row_max(p, c):
                wait(sp, s_mr, p, NC, c)
                sp.dma_start(terms2[64:65, 2 * NC + c, :, :].rearrange("o a t -> o (a t)")
                             .rearrange("o (r t) -> o r t", t=TB).bitcast(f32),
                             mrow[:, :].bitcast(f32)).then_inc(d_m, 16)

            def spread(p, c):
                wait(sp, s_lr, p, NC, c)
                wait(sp, s_rc, p, NC, c - 1)
                for a in range(2):
                    sp.dma_start(rcol[D * a:D * a + D, :], lrow[D * a:D * a + 1, :]
                                 .rearrange("o (r t) -> o r t", t=8)).then_inc(d_l, 16)
                wait(sp, s_rc, p, NC, c)
                wait(sp, d_b, p, NC, c - 1, 32)
                sp.dma_start(irow[:, :].rearrange("o (r t) -> o r t", t=8), icol[:, :]).then_inc(d_i, 16)
                wait(sp, d_i, p, NC, c, 16)
                wait(sp, s_yn, p, NC, c - 1)
                for a in range(2):
                    sp.dma_start(rb[D * a:D * a + D, :], irow[0:1, a * CH:(a + 1) * CH]
                                 .unsqueeze(1).to_broadcast([1, D, CH])).then_inc(d_b, 16)

            zero = Pair(0)
            operands(zero, 0)
            operands(zero, 1)
            wait(sp, s_wl, zero, 1, 0)
            sp.dma_start(w_raw[:, :], w_qkv[1]).then_inc(d_w, 16)
            row_max(zero, 0)
            operands(zero, 2)
            row_max(zero, 1)
            operands(zero, 3)

            def body(p):
                more = p.i is not None or p.n < PAIRS - 1
                nxt = p.ahead(1)
                if more:
                    first = 1 + p.n if p.i is None else p.i * 2 + (1 + p.n)
                if more and p.n:
                    wait(sp, s_wl, p, 1, 0)
                    sp.dma_start(w_raw[:, :], w_qkv[bass.ds(first, 1), :, :].rearrange("o c n -> (o c) n"))\
                        .then_inc(d_w, 16)
                if p.n:
                    spread(p.ahead(-1), 3)
                if p.n:
                    row_max(p, 2)
                if more:
                    operands(nxt, 0)
                if not p.n:
                    row_max(p, 2)
                if more:
                    wait(sp, s_op, p.ahead(-1), NC, NC - 1)
                    sp.dma_start(wo[:, nxt.parity(), :],
                                 w_o.rearrange("(n r) c -> n r c", r=128)[bass.ds(first, 1), :, :]
                                 .rearrange("o r c -> (o r) c")).then_inc(d_wo, 16)
                spread(p, 0)
                if more:
                    operands(nxt, 1)
                spread(p, 1)
                row_max(p, 3)
                if more:
                    operands(nxt, 2)
                    row_max(nxt, 0)
                spread(p, 2)
                if more:
                    row_max(nxt, 1)
                    operands(nxt, 3)

            over_pairs(nc, sp, body)
            for i in range(2 * NC, 3 * NC + 1):
                xs, _ = span(i)
                sp.wait_ge(f_x, i - NC + 1)
                sp.dma_start(out_t[:, xs], x[:, xs]).then_inc(d_out, 16)
            sp.wait_ge(d_out, 16 * (NC + 1))

        @block.tensor
        def _(pe):
            def normal(step, i):
                xs, own = span(i)
                blocks = (own.stop - own.start) // TB
                if step == "mean":
                    if i < NC:
                        pe.wait_ge(d_in[i], 16)
                    elif i < 2 * NC:
                        pe.wait_ge(f_x, i - NC + 1)
                    else:
                        pe.wait_ge(s_xa, NC * (PAIRS - 1) + i - 2 * NC + 1)
                        if i == 2 * NC:
                            pe.wait_ge(s_rd, NM * PAIRS)
                        else:
                            pe.wait_ge(f_x, min(i - NC, 2 * NC - 1))
                    pe.matmul(ps[:, norm_bank(i), own], mean_w[:, :], x[:, xs],
                              start=True, stop=True).then_inc(l_mean, 1)
                elif step == "var":
                    pe.wait_ge(l_sq, i + 1)
                    for b in range(own.start // TB, own.start // TB + blocks):
                        col = own.start + b - own.start // TB
                        mm = pe.matmul(ps[:, norm_bank(i), col:col + 1], sq(i)[:, b * TB:(b + 1) * TB],
                                       mean_w[:, 0:1], start=True, stop=True)
                    mm.then_inc(l_var, 1)
                else:
                    pe.wait_ge(l_rs, i + 1)
                    for b in range(blocks):
                        t = BPC * i + b
                        to = own.start + b * TB
                        mm = pe.matmul(ps[:, norm_bank(i), to:to + TB],
                                       rinv[:, t:t + 1].to_broadcast([128, 128]), ident[:, :],
                                       start=True, stop=True)
                    mm.then_inc(l_sp, 1)

            def feed_forward(step, i):
                _, own = span(norm_of(i))
                if step == "mixed":
                    for n in range(2):
                        pe.wait_ge(f_mix, 2 * i + n + 1)
                        if 0 < i < NC:
                            pe.wait_ge((f_r, f_k)[n], i)
                        pe.matmul(ps[:, mix_bank(i, n), own], wf[:, n, :], mixed(i, n)[:, own],
                                  start=True, stop=True).then_inc(f_z, 1)
                else:
                    pe.wait_ge(f_ka, i + 1)
                    if i >= NC:
                        pe.wait_ge(f_r, i + 1)
                    elif i:
                        pe.wait_ge(f_g, i)
                    pe.matmul(ps[:, value_bank(i), own], wf[:, 2, :], act_of(i)[:, own],
                              start=True, stop=True)\
                        .then_inc(f_v, 1)

            tasks = []

            def bank_free(bank):
                before = [t for t in tasks if bank_of(*t).offset == bank.offset]
                if before:
                    tasks.remove(before[0])
                    kind, p, c, k = before[0]
                    if kind == PROJ:
                        if k < 2:
                            wait(pe, s_lo, p, 8, 2 * c + k)
                        else:
                            wait(pe, s_hv, p, 12, 3 * c + 2)
                    else:
                        wait(pe, {MROW: s_mr, SUMS: s_lr, OUTP: s_xa}[kind], p, NC, c)

            def task(kind, p, c, k):
                bank = bank_of(kind, p, c, k)
                bank_free(bank)
                tasks.append((kind, p, c, k))
                if kind == PROJ:
                    if p.i is None and p.n == 0 and k == 0:
                        pe.wait_ge(l_hi, c + 1)
                        pe.wait_ge(l_lo, c + 1)
                    if c == 0 and k == 0:
                        wait(pe, s_wl, p, 1, 0)
                    if k < 2:
                        for n, (w, xx) in enumerate(((wh, xh), (wl, xh), (wh, xl))):
                            mm = pe.matmul(bank[:, :], w[:, k * 128:(k + 1) * 128], xx[:, chunk(c)],
                                           start=n == 0, stop=n == 2)
                    else:
                        for b in range(BPC):
                            t = BPC * c + b
                            for n, (w, xx) in enumerate(((wh, xh), (wl, xh), (wh, xl))):
                                mm = pe.matmul(bank[:, b * TB:(b + 1) * TB], xx[:, t * TB:(t + 1) * TB],
                                               w[:, 256:384], start=n == 0, stop=n == 2)
                    mm.then_inc(s_pj, 1)
                elif kind == MROW:
                    wait(pe, s_nm, p, NC, c)
                    pe.transpose(misc[0:8, 0:128], neg[:, c % 2, :], ident[:, :]).then_inc(s_mt, 1)
                elif kind == SUMS:
                    wait(pe, s_ac, p, NU, LAST[c])
                    wait(pe, s_pa, p, NU, LAST[c])
                    for a in range(2):
                        mm = pe.matmul(misc[D * a:D * a + D, :], ones[:, :], part[:, c % 2, a, :],
                                       start=True, stop=True)
                    mm.then_inc(s_sum, 1)
                else:
                    wait(pe, s_yn, p, NC, c)
                    wait(pe, d_wo, p, 1, 0, 16)
                    pe.matmul(misc[:, :], wo[:, p.parity(), :], yn[:, :], start=True, stop=True)\
                        .then_inc(s_op, 1)

            def piece(p, g):
                c, b, a, k = PIECES[g]
                number, back = max_bank(p, g)
                wait(pe, s_rd, p, NM, g - back)
                if (b, a, k) == (0, 0, 0):
                    wait(pe, d_a[c], p, 1, 0, 96)
                width = CH if k < c else (b + 1) * TB
                bank = ps[:, number, :]
                mm = pe.matmul(bank[:, 0:width], terms1[:, 2 * NC + c, a, b * TB:(b + 1) * TB],
                               terms1[:, p.parity() * NC + k, a, 0:width], start=True, stop=k < c)
                if k == c:
                    mm = pe.matmul(bank[:, width - TB:width], identb[:, :], above[:, :],
                                   start=False, stop=True)
                mm.then_inc(s_mx, 1)

            def scores(p, u, a):
                c, j, off = UNITS[u]
                n = 2 * u + a
                if p.i is None and p.n == 0 and n < ST_RING:
                    wait(pe, s_rd, p, NM, LEAD_0 - 1)
                if j == 0 and a == 0:
                    wait(pe, d_m, p, NC, c, 16)
                wait(pe, s_ex, p, 2 * NU, n - ST_RING if n >= ST_RING else n - 2)
                bank = ps[:, st_bank(n), :]
                blk = slice(j % BPC * TB, (j % BPC + 1) * TB)
                pe.matmul(bank[:, off:CH], terms1[:, p.parity() * NC + j // BPC, a, blk],
                          terms1[:, 2 * NC + c, a, off:CH], start=True, stop=False)
                pe.matmul(bank[:, off:CH], terms2[:, p.parity() * NC + j // BPC, a, blk],
                          terms2[:, 2 * NC + c, a, off:CH], start=False, stop=True).then_inc(s_st, 1)

            def weighted(p, u):
                c, j, off = UNITS[u]
                if j == 0:
                    wait(pe, s_yr, p, NC, c - 2)
                    wait(pe, s_hv, p, 12, 3 * c + 2)
                wait(pe, s_ex, p, 2 * NU, 2 * u + 1)
                if j >= BPC * c:
                    wait(pe, s_mk, p, NT, BPC * c + j % BPC)
                for a in range(2):
                    mm = pe.matmul(ps[D * a:D * a + D, 3 + c % 2, off:CH],
                                   vals[:, p.parity() * NT + j, D * a:D * a + D],
                                   prob[:, slot_of(u), a, off:CH],
                                   start=j == 0, stop=u == LAST[c])
                mm.then_inc(s_pv, 1)

            zero = Pair(0)
            pe.wait_ge(s_set, 5)
            for what, *rest in PE_START:
                if what in ("mean", "var", "spread"):
                    normal(what, rest[0])
                elif what in ("mixed", "value"):
                    if rest[0] == 0 and what == "mixed":
                        pe.wait_ge(d_c, 48)
                    feed_forward(what, rest[0])
                elif what == "max":
                    if rest[0] == 0:
                        pe.wait_ge(f_x, NC)
                    for g in range(*rest):
                        piece(zero, g)
                elif what == "proj":
                    task(PROJ, zero, *rest)
                else:
                    task(MROW, zero, rest[0], 0)
            pe.wait_ge(s_set, 6)

            def end_step(step, c):
                if step in ("mixed", "value"):
                    feed_forward(step, NC + c)
                else:
                    normal(step, 2 * NC + c)

            def body(p):
                more = p.i is not None or p.n < PAIRS - 1
                side = slots_of(p, SIDE, SIDE_0)
                for u in range(NU):
                    pieces = pieces_in(p, u)
                    scores(p, u, 0)
                    for ahead, g in pieces[:1]:
                        piece(ahead, g)
                    scores(p, u, 1)
                    for ahead, g in pieces[1:]:
                        piece(ahead, g)
                    if u % 2 == 0:
                        for back in (2, 1):
                            if u:
                                weighted(p, u - back)
                            elif p.n > 0:
                                weighted(p.ahead(-1), NU - back)
                    if u in side:
                        kind, k, c, n = side[u]
                        task(kind, p.ahead(k), c, n)
                    if not more:
                        for step, c in end_steps(PE_END, u):
                            end_step(step, c)
                if more:
                    tasks.clear()
                    kind, k, c, n = SIDE[max(SIDE)]
                    tasks.append((kind, p.ahead(k), c, n))

            over_pairs(nc, pe, body)
            last = Pair(PAIRS - 1)
            weighted(last, NU - 2)
            weighted(last, NU - 1)
            task(SUMS, last, NC - 1, 0)
            for h in range(2):
                pe.wait_ge(s_yn, NC * PAIRS + h)
                own = slice(h * HALF, (h + 1) * HALF)
                pe.matmul(ps[:, 2 + h, own], wo[:, last.parity(), :], yn[:, own], start=True, stop=True)\
                    .then_inc(s_op, 1)
            for step, h in PE_LAST:
                end_step(step, NC - 1 + h)

        @block.scalar
        def _(act):
            def step(what, i):
                is_norm = what in ("square", "deviation")
                xs, own = span(i if is_norm else norm_of(i))
                if what == "square":
                    act.wait_ge(l_xc, i + 1)
                    if i >= 2:
                        act.wait_ge(l_var, i - 1 if i < 2 * NC else 3 * NC - 1)
                    act.activation(sq(i)[:, own], xc(i)[:, own], ACT.Square).then_inc(l_sq, 1)
                elif what == "deviation":
                    act.wait_ge(l_var, i + 1)
                    n = (own.stop - own.start) // TB
                    act.activation(rinv[:, BPC * i:BPC * i + n],
                                   ps[:, norm_bank(i), own.start:own.start + n], ACT.Sqrt,
                                   bias=eps[:, 0:1]).then_inc(l_std, 1)
                elif what == "high":
                    act.wait_ge(l_xn, NC + i + 1)
                    act.activation(xh[:, xs], xn[:, 1 + xs.start:1 + xs.stop], ACT.Copy)\
                        .then_inc(l_hi, 1)
                elif what == "previous":
                    act.wait_ge(s_omu, 1)
                    act.wait_ge(l_xn, norm_of(i) + 1)
                    if i >= 2:
                        act.wait_ge(f_z, 2 * (i - 1 if i < NC else 2 * NC - 1))
                    for n in range(2):
                        act.activation(mixed(i, n)[:, own], xn[:, xs], ACT.Copy,
                                       scale=omu[:, n:n + 1]).then_inc(f_t, 1)
                elif what == "gate":
                    act.wait_ge(f_z, 2 * i + 1)
                    if i >= 2:
                        act.wait_ge(f_x, i - 1 if i < NC else min(i, 2 * NC - 1))
                    act.activation(gate_of(i)[:, own], ps[:, mix_bank(i, 0), own], ACT.Tanh, scale=0.5)\
                        .then_inc(f_r, 1)
                else:
                    step("gate", i)
                    act.wait_ge(f_z, 2 * i + 2)
                    relu = relu_of(i)[:, own]
                    if i >= 2:
                        act.wait_ge(f_v, i - 1 if i < NC else 2 * NC - 1)
                    if i:
                        act.wait_ge(f_ka, i if i < NC else 2 * NC - 1)
                    act.activation(relu, ps[:, mix_bank(i, 1), own], ACT.Relu).then_inc(f_k, 1)
                    act.wait_ge(f_k, i + 1)
                    act.activation(act_of(i)[:, own], relu, ACT.Square).then_inc(f_ka, 1)

            def split_weights(p):
                wait(act, d_w, p, 1, 0, 16)
                wait(act, s_pj, p.ahead(-1), 12, 11)
                act.activation(wh[:, :], w_raw[:, :], ACT.Copy).then_inc(s_wh, 1)

            def task(kind, p, c, k):
                bank = bank_of(kind, p, c, k)
                if kind == PROJ:
                    wait(act, s_pj, p, 12, 3 * c + k)
                    if k < 2:
                        if k == 0:
                            if c >= 2:
                                wait(act, d_a[c - 2], p, 1, 0, 96)
                            else:
                                wait(act, d_a[c + 2], p.ahead(-1), 1, 0, 96)
                        act.activation(split[:, c % 2, (QH, KH)[k], :], bank[:, :], ACT.Copy)\
                            .then_inc(s_hv, 1)
                    else:
                        wait(act, s_pv, p.ahead(-2), NU, NU - 1)
                        v0 = p.parity() * NT + BPC * c
                        act.activation(vals[:, v0:v0 + BPC, :].rearrange("p b c -> p (b c)"), bank[:, :],
                                       ACT.Copy).then_inc(s_hv, 1)
                elif kind == MROW:
                    wait(act, s_mt, p, NC, c)
                    wait(act, d_m, p, NC, c - 1, 16)
                    act.activation(mrow[:, :], misc[0:8, 0:128], ACT.Copy).then_inc(s_mr, 1)
                elif kind == SUMS:
                    wait(act, s_sum, p, NC, c)
                    wait(act, d_l, p, NC, c - 1, 32)
                    act.activation(lrow[:, :], misc[:, :], ACT.Copy).then_inc(s_lr, 1)
                    wait(act, s_pv, p, NU, LAST[c])
                    wait(act, s_yn, p, NC, c - 1)
                    act.activation(yraw[:, :], ps[:, 3 + c % 2, :], ACT.Copy).then_inc(s_yr, 1)

            zero = Pair(0)
            act.wait_ge(s_set, 5)
            act.activation(warm[:, 0:1], eps[:, :], ACT.Sqrt)
            for what, *rest in ACT_START:
                if what == "weights":
                    split_weights(zero)
                elif what == "proj":
                    task(PROJ, zero, *rest)
                elif what == "mrow":
                    task(MROW, zero, rest[0], 0)
                else:
                    step(what, rest[0])

            def body(p):
                more = p.i is not None or p.n < PAIRS - 1
                side = slots_of(p, SIDE, SIDE_0)
                for u in range(NU):
                    c, j, off = UNITS[u]
                    wait(act, s_pv, p, NU, u - NP)
                    wait(act, s_ac, p, NU, u - NP)
                    wait(act, s_pa, p, NU, u - NP)
                    for a in range(2):
                        wait(act, s_st, p, 2 * NU, 2 * u + a)
                        act.activation(prob[:, slot_of(u), a, off:CH], ps[:, st_bank(2 * u + a), off:CH],
                                       ACT.Exp, scale=SCALE).then_inc(s_ex, 1)
                    if u in side:
                        kind, k, cc, n = side[u]
                        task(kind, p.ahead(k), cc, n)
                    if u == 3 and more:
                        split_weights(p.ahead(1))
                    if not more:
                        for what, c in end_steps(ACT_END, u):
                            step(what, (NC if what == "gate" else 2 * NC) + c)

            over_pairs(nc, act, body)
            act.activation(warm[:, 1:2], eps[:, :], ACT.Sqrt)
            for what, h in ACT_LAST:
                step(what, (3 * NC if what in ("square", "deviation") else 2 * NC) - 1 + h)
                if (what, h) == ("deviation", 1):
                    act.activation(warm[:, 2:3], eps[:, :], ACT.Tanh)

        @block.vector
        def _(dve):
            def step(what, i):
                norm = what in ("center", "square", "inverse", "scale", "low")
                xs, own = span(i if norm else norm_of(i))
                after_token = slice(1 + xs.start, 1 + xs.stop)
                if what == "center":
                    if i >= NC:
                        if i < 2 * NC:
                            dve.wait_ge(f_x, i - NC + 1)
                        else:
                            dve.wait_ge(s_xa, NC * (PAIRS - 1) + i - 2 * NC + 1)
                    dve.wait_ge(l_mean, i + 1)
                    dve.tensor_tensor(xc(i)[:, own], x[:, xs], ps[:, norm_bank(i), own], ALU.subtract)\
                        .then_inc(l_xc, 1)
                elif what == "square":
                    dve.wait_ge(l_xc, i + 1)
                    dve.tensor_tensor(sq(i), xc(i), xc(i), ALU.mult).then_inc(l_sq, 1)
                elif what == "inverse":
                    dve.wait_ge(l_std, i + 1)
                    n = (own.stop - own.start) // TB
                    dve.reciprocal(rinv[:, BPC * i:BPC * i + n], rinv[:, BPC * i:BPC * i + n])\
                        .then_inc(l_rs, 1)
                elif what == "scale":
                    dve.wait_ge(l_xc, i + 1)
                    dve.wait_ge(l_sp, i + 1)
                    if NC <= i < 2 * NC - 1:
                        dve.wait_ge(f_t, 2 * (i - NC) + 4)
                    dve.tensor_tensor(xn[:, after_token], xc(i)[:, own],
                                      ps[:, norm_bank(i), own], ALU.mult).then_inc(l_xn, 1)
                elif what == "low":
                    dve.wait_ge(l_hi, i + 1)
                    dve.tensor_tensor(xl[:, xs], xn[:, after_token], xh[:, xs].bitcast(f32),
                                      ALU.subtract).then_inc(l_lo, 1)
                elif what == "previous":
                    dve.wait_ge(l_xn, norm_of(i) + 1)
                    for n in range(2):
                        dve.tensor_scalar(mixed(i, n)[:, own], xn[:, xs], omu[:, n:n + 1],
                                          None, ALU.mult).then_inc(f_t, 1)
                elif what == "mix":
                    for n in range(2):
                        dve.wait_ge(f_t, 2 * i + n + 1)
                        dve.scalar_tensor_tensor(mixed(i, n)[:, own], xn[:, after_token],
                                                 mu[:, n:n + 1], mixed(i, n)[:, own], ALU.mult,
                                                 ALU.add)\
                            .then_inc(f_mix, 1)
                elif what == "relu2":
                    dve.wait_ge(f_z, 2 * i + 2)
                    dve.tensor_scalar(piece_of(lflat, 3), ps[:, mix_bank(i, 1), :], 0.0, None, ALU.max)\
                        .then_inc(f_k, 1)
                    dve.wait_ge(f_k, i + 1)
                    dve.tensor_tensor(act_of(i), piece_of(lflat, 3), ps[:, mix_bank(i, 1), :],
                                      ALU.mult).then_inc(f_ka, 1)
                else:
                    dve.wait_ge(f_v, i + 1)
                    dve.wait_ge(f_r, i + 1)
                    if i:
                        dve.wait_ge(f_x, min(i, 2 * NC - 1))
                    dve.scalar_tensor_tensor(gated(i)[:, own], gate_of(i)[:, own], 1.0,
                                             ps[:, value_bank(i), own], ALU.add, ALU.mult)\
                        .then_inc(f_g, 1)
                    dve.wait_ge(f_g, i + 1)
                    dve.scalar_tensor_tensor(x[:, xs], gated(i)[:, own], 0.25, x[:, xs], ALU.mult,
                                             ALU.add).then_inc(f_x, 1)

            def split_weights(p):
                wait(dve, s_wh, p, 1, 0)
                wait(dve, s_pj, p.ahead(-1), 12, 11)
                dve.tensor_tensor(wl[:, :], w_raw[:, :], wh[:, :].bitcast(f32), ALU.subtract)\
                    .then_inc(s_wl, 1)

            def task(kind, p, c, k):
                if kind == PROJ and k < 2:
                    wait(dve, s_hv, p, 12, 3 * c + k)
                    if k == 0:
                        if c >= 2:
                            wait(dve, d_a[c - 2], p, 1, 0, 96)
                        else:
                            wait(dve, d_a[c + 2], p.ahead(-1), 1, 0, 96)
                    dve.tensor_tensor(split[:, c % 2, (QL, KL)[k], :], bank_of(kind, p, c, k)[:, :],
                                      split[:, c % 2, (QH, KH)[k], :].bitcast(f32),
                                      ALU.subtract).then_inc(s_lo, 1)
                elif kind == RECIP:
                    wait(dve, d_l, p, NC, c, 32)
                    wait(dve, d_i, p, NC, c - 1, 16)
                    dve.reciprocal(icol[:, :], rcol[:, :]).then_inc(s_rc, 1)
                elif kind == NORM:
                    wait(dve, d_b, p, NC, c, 32)
                    wait(dve, s_yr, p, NC, c)
                    wait(dve, s_op, p, NC, c - 1)
                    dve.tensor_tensor(yn[:, :], yraw[:, :], rb[:, :], ALU.mult).then_inc(s_yn, 1)
                elif kind == OUTP:
                    wait(dve, s_op, p, NC, c)
                    wait(dve, s_xa, p, NC, c - NC)
                    dve.tensor_tensor(x[:, chunk(c)], x[:, chunk(c)], misc[:, :], ALU.add).then_inc(s_xa, 1)

            def piece(p, g):
                c, b, a, k = PIECES[g]
                width = CH if k < c else (b + 1) * TB
                wait(dve, s_mx, p, NM, g)
                dve.tensor_reduce(most[:, c % 2, 4 * a + b, k:k + 1], ps[:, max_bank(p, g)[0], 0:width], AX.X,
                                  ALU.max).then_inc(s_rd, 1)

            def maxima(p, c):
                wait(dve, s_rd, p, NM, max(g for g in range(NM) if PIECES[g][0] == c))
                wait(dve, s_mt, p, NC, c - 2)
                dve.tensor_reduce(neg[:, c % 2, :], most[:, c % 2, :, 0:c + 1], AX.X, ALU.max,
                                  negate=True).then_inc(s_nm, 1)

            def sums(p, u):
                c, j, off = UNITS[u]
                if j == 0 or u == LAST[c]:
                    return
                s, s0 = slot_of(u), slot_of(u - 1)
                wait(dve, s_ex, p, 2 * NU, 2 * u + 1)
                if j >= BPC * c:
                    wait(dve, s_mk, p, NT, BPC * c + j % BPC)
                if j == 1:
                    wait(dve, s_sum, p, NC, c - 2)
                    if off:
                        dve.tensor_copy(part[:, c % 2, :, 0:off], prob[:, s0, :, 0:off])
                    dve.tensor_tensor(part[:, c % 2, :, off:POOL_FROM], prob[:, s0, :, off:POOL_FROM],
                                      prob[:, s, :, off:POOL_FROM], ALU.add).then_inc(s_ac, 2)
                else:
                    wait(dve, s_ac, p, NU, u - 1)
                    dve.tensor_tensor(part[:, c % 2, :, off:POOL_FROM], part[:, c % 2, :, off:POOL_FROM],
                                      prob[:, s, :, off:POOL_FROM], ALU.add)\
                        .then_inc(s_ac, 2 if u == LAST[c] - 1 else 1)

            zero = Pair(0)
            dve.memset(vz[:, 0:1], 0.0)
            dve.wait_ge(s_set, 5)
            dve.tensor_copy(identb[:, :], ident[:, :])
            for what, *rest in DVE_START:
                if what == "weights":
                    split_weights(zero)
                elif what == "max":
                    for g in range(*rest):
                        piece(zero, g)
                elif what == "neg":
                    maxima(zero, rest[0])
                elif what == "proj":
                    task(PROJ, zero, *rest)
                else:
                    step(what, rest[0])
                if (what, rest) == ("center", [NC - 1]):
                    dve.wait_ge(d_x, 32)
                    dve.tensor_scalar(omu[:, :], mu[:, :], -1.0, 1.0, ALU.mult, ALU.add)\
                        .then_inc(s_omu, 1)

            def end_step(what, c):
                norm = what in ("center", "square", "inverse", "scale")
                step(what, (2 * NC if norm else NC) + c)

            def side(p, u, more):
                for steps in (slots_of(p, SIDE, SIDE_0), slots_of(p, DVE_SIDE)):
                    if u in steps:
                        kind, k, c, n = steps[u]
                        task(kind, p.ahead(k), c, n)
                if u in slots_of(p, MAXIMA, MAXIMA_0):
                    c, k = slots_of(p, MAXIMA, MAXIMA_0)[u]
                    maxima(p.ahead(k), c)
                if u == 3 and more:
                    split_weights(p.ahead(1))
                if not more:
                    for what, c in end_steps(DVE_END, u):
                        end_step(what, c)

            def body(p):
                more = p.i is not None or p.n < PAIRS - 1
                for u in range(NU):
                    pieces = pieces_in(p, u)
                    for ahead, g in pieces[:1]:
                        piece(ahead, g)
                    if u:
                        side(p, u - 1, more)
                    for ahead, g in pieces[1:]:
                        piece(ahead, g)
                    if u and u % 2 == 0:
                        sums(p, u - 2)
                        sums(p, u - 1)
                sums(p, NU - 2)
                sums(p, NU - 1)
                side(p, NU - 1, more)

            over_pairs(nc, dve, body)
            last = Pair(PAIRS - 1)
            c = NC - 1
            halves = [slice(h * HALF, (h + 1) * HALF) for h in range(2)]
            wait(dve, s_sum, last, NC, c)
            wait(dve, s_pv, last, NU, NU - 1)
            wait(dve, s_op, last, NC, c - 1)
            for h, own in enumerate(halves):
                dve.reciprocal(rb[:, own], misc[:, own]).then_inc(s_rc, 1)
                wait(dve, s_rc, last, NC, c + h)
                dve.tensor_tensor(yn[:, own], ps[:, 3 + c % 2, own], rb[:, own], ALU.mult)\
                    .then_inc(s_yn, 1)
            for h, own in enumerate(halves):
                xs, _ = span(3 * NC - 1 + h)
                wait(dve, s_op, last, NC, c + h)
                dve.tensor_tensor(x[:, xs], x[:, xs], ps[:, 2 + h, own], ALU.add).then_inc(s_xa, 1)
            for what, h in DVE_LAST:
                end_step(what, c + h)

        @block.gpsimd
        def _(pool):
            pool.memset(ident[:, :], 0.0).then_inc(s_pool, 1)
            pool.memset(above[:, :], 0.0).then_inc(s_pool, 1)
            pool.memset(ones[:, :], 1.0).then_inc(s_set, 1)
            pool.memset(mean_w[:, :], 1.0 / C).then_inc(s_set, 1)
            pool.memset(eps[:, :], EPS).then_inc(s_set, 1)
            pool.wait_ge(s_pool, 2)
            pool.wait_ge(s_set, 1)
            pool.affine_select(out=ident[:, :], in_=ident[:, :], compare_op=ALU.not_equal, fill=1.0,
                               base=0, pattern=[[-1, 128]], channel_multiplier=1).then_inc(s_set, 1)
            pool.affine_select(out=above[:, :], in_=above[:, :], compare_op=ALU.is_ge, fill=-1e30,
                               base=0, pattern=[[-1, 128]], channel_multiplier=1).then_inc(s_set, 1)
            pool.wait_ge(s_set, 5)
            pool.memset(terms2[64:65, 0:2 * NC, :, :].bitcast(f32), 1.0).then_inc(s_set, 1)
            pool.wait_ge(s_set, 6)

            def body(p):
                for u in range(NU):
                    c, j, off = UNITS[u]
                    s, s0 = slot_of(u), slot_of(u - 1)
                    lo = max(off, POOL_FROM)
                    if j >= BPC * c:
                        wait(pool, s_ex, p, 2 * NU, 2 * u + 1)
                        pool.tensor_tensor(gate[:, u:u + 1], ones[:, 0:1], ones[:, 0:1], ALU.add)
                        diag = prob[:, s, :, off:off + TB]
                        pool.affine_select(out=diag, in_=diag, compare_op=ALU.is_ge, fill=0.0, base=0,
                                           pattern=[[0, 2], [1, TB]], channel_multiplier=-1)\
                            .then_inc(s_mk, 1)
                    if j == 0:
                        continue
                    wait(pool, s_ex, p, 2 * NU, 2 * u + 1)
                    if j >= BPC * c:
                        wait(pool, s_mk, p, NT, BPC * c + j % BPC)
                    if j == 1:
                        wait(pool, s_sum, p, NC, c - 2)
                        pool.tensor_tensor(part[:, c % 2, :, lo:CH], prob[:, s0, :, lo:CH],
                                           prob[:, s, :, lo:CH], ALU.add).then_inc(s_pa, 2)
                    else:
                        wait(pool, s_pa, p, NU, u - 1)
                        pool.tensor_tensor(part[:, c % 2, :, lo:CH], part[:, c % 2, :, lo:CH],
                                           prob[:, s, :, lo:CH], ALU.add).then_inc(s_pa, 1)

            over_pairs(nc, pool, body)


def kernel(**inputs):
    import concourse.bacc as _bacc
    from concourse import mybir as _mybir
    from concourse.bass_utils import run_bass_kernel_spmd as _run

    def a(name):
        return np.asarray(inputs["L0_" + name])

    def pairs(w):
        return w.reshape(PAIRS, 2 * D, C).transpose(0, 2, 1)

    arrays = {
        "x_t": a("attn_x_q").reshape(T, C).T,
        "w_qkv": np.concatenate([pairs(a("attn_w_q")), pairs(a("attn_w_k")), pairs(a("attn_w_v"))], axis=2),
        "w_o": a("attn_w_o"),
        "w_r": a("ffn_W_r").T, "w_k": a("ffn_W_k").T, "w_v": a("ffn_W_v").T,
        "mu_r": a("ffn_mu_r").reshape(C, 1), "mu_k": a("ffn_mu_k").reshape(C, 1),
    }
    arrays = {k: np.ascontiguousarray(v) for k, v in arrays.items()}
    nc = _bacc.Bacc("TRN2", target_bir_lowering=False, num_devices=1)
    args = [nc.dram_tensor(k, v.shape, _mybir.dt.from_np(v.dtype), kind="ExternalInput").ap()
            for k, v in arrays.items()]
    args.append(nc.dram_tensor("out_t", (C, T), _mybir.dt.float32, kind="ExternalOutput").ap())
    nc.disable_value_cache = True
    macaron_kernel(nc, *args)
    r = _run(nc, [arrays], core_ids=[0])
    return np.ascontiguousarray(r.results[0]["out_t"].T).reshape(1, T, C)
```
